# Optimizing a Trainium2 kernel written in Bass

```python
import numpy as np
import jax
import jax.numpy as jnp

def _softmax(x, axis=-1):
    return jax.nn.softmax(x, axis=axis)

def _gelu(x):
    return jax.nn.gelu(x, approximate=True)

def _silu(x):
    return jax.nn.silu(x)

def _sigmoid(x):
    return jax.nn.sigmoid(x)

def _layernorm(x, axis=-1, eps=1e-05):
    m = jnp.mean(x, axis=axis, keepdims=True)
    v = jnp.var(x, axis=axis, keepdims=True)
    return (x - m) / jnp.sqrt(v + eps)

def _scatter_add(tgt, idx, src, axis=0):
    return tgt.at[idx].add(src)

def _segment_sum(src, seg, n):
    return jax.ops.segment_sum(src, seg, n)
kernel_name = 'mk_xattn_ffn_d2_seqx_r8_853c65'

def setup_inputs(seed: int=0):
    np.random.seed(seed)
    _w = jnp.asarray

    def _rec_inputs():
        import jax
        import jax.numpy as jnp
        _rk = jax.random.key(seed)
        x = -0.0003929 + 0.9999 * jax.random.normal(jax.random.fold_in(_rk, 1), (4, 256, 256), jnp.float32)
        _lenS = 256 - jax.random.randint(jax.random.fold_in(_rk, 7), (4,), 0, max(1, 256 // 4) + 1, jnp.int32)
        _lenS2 = 256 - jax.random.randint(jax.random.fold_in(_rk, 8), (4,), 0, max(1, 256 // 4) + 1, jnp.int32)
        _ctx_2048P = jax.random.normal(jax.random.fold_in(_rk, 11), (4, 16, 256), jnp.float32)
        _ctx_2048c = jax.random.dirichlet(jax.random.fold_in(_rk, 511), 0.3 * jnp.ones((16,), jnp.float32), (4, 256))
        _ctx_2048t = jnp.einsum('bsk,bkd->bsd', _ctx_2048c, _ctx_2048P)
        _ctx_2048t = _ctx_2048t * jax.lax.rsqrt(jnp.mean(jnp.square(_ctx_2048t)) + 1e-12) * 0.953939
        ctx_2048 = -0.000514642 + 1.00011 * (_ctx_2048t + 0.3 * jax.random.normal(jax.random.fold_in(_rk, 611), (4, 256, 256), jnp.float32))
        _validS = jnp.arange(256)[None, :] < _lenS[:, None]
        _validS2 = jnp.arange(256)[None, :] < _lenS2[:, None]
        _causal = jnp.tril(jnp.ones((256, 256), dtype=bool))
        mask_BxS2_ik0 = jnp.where(jnp.broadcast_to(_validS2[:, :], (4, 256)), 0, 1).astype(jnp.int32)
        return (x, ctx_2048, mask_BxS2_ik0)
    x, ctx_2048, mask_BxS2_ik0 = _rec_inputs()

    def _L0_xattn_setup():
        import jax, jax.numpy as jnp
        import numpy as np
        import math
        H = 256
        NH = 16
        HD = H // NH
        EPS_LN = 1e-05
        RES_SCALE_MAX = 0.3

        def _nan_clean(x, lim=10000.0):
            return jnp.nan_to_num(x, nan=0.0, posinf=lim, neginf=-lim)
        key = jax.random.key(seed)
        ks = jax.random.split(key, 12)
        B, S, T = (4, 256, 32)
        std = 1.0 / math.sqrt(H)
        return {'hidden_states': jax.random.normal(ks[0], (B, S, H), jnp.float32), 'audio_tokens': jax.random.normal(ks[1], (B, T, H), jnp.float32), 'attention_mask': jax.random.randint(ks[2], (B, T), 0, 2, jnp.int32), 'Wq': jax.random.normal(ks[3], (H, H), jnp.float32) * std, 'bq': jnp.zeros((H,), jnp.float32), 'Wk': jax.random.normal(ks[4], (H, H), jnp.float32) * std, 'bk': jnp.zeros((H,), jnp.float32), 'Wv': jax.random.normal(ks[5], (H, H), jnp.float32) * std, 'bv': jnp.zeros((H,), jnp.float32), 'Wo': jax.random.normal(ks[6], (H, H), jnp.float32) * std, 'bo': jnp.zeros((H,), jnp.float32), 'ln_gamma': jnp.ones((H,), jnp.float32), 'ln_beta': jnp.zeros((H,), jnp.float32), 'residual_scale': jnp.float32(0.05)}
    _L0_xattn_all = _L0_xattn_setup()
    _L0_xattn_in = {k: v for k, v in _L0_xattn_all.items() if k in ('Wq', 'bq', 'Wk', 'bk', 'Wv', 'bv', 'Wo', 'bo', 'ln_gamma', 'ln_beta', 'residual_scale')}
    del _L0_xattn_all

    def _L0_ffn_setup():
        import jax, jax.numpy as jnp
        import numpy as np
        TOP_K = 2
        LORA_SCALE = 32.0 / 16.0
        key = jax.random.key(seed)
        ks = jax.random.split(key, 11)
        B, S, D, F, E, R = (4, 128, 256, 704, 8, 16)
        sd, sf = (1.0 / np.sqrt(D), 1.0 / np.sqrt(F))
        return {'x': jax.random.normal(ks[0], (B, S, D), jnp.float32), 'gate_w': jax.random.normal(ks[1], (E, D), jnp.float32) * 0.02, 'w1': jax.random.normal(ks[2], (F, D), jnp.float32) * sd, 'w3': jax.random.normal(ks[3], (F, D), jnp.float32) * sd, 'w2': jax.random.normal(ks[4], (D, F), jnp.float32) * sf, 'a1': jax.random.normal(ks[5], (E, R, D), jnp.float32) * sd, 'b1': jax.random.normal(ks[6], (E, F, R), jnp.float32) * 0.01, 'a3': jax.random.normal(ks[7], (E, R, D), jnp.float32) * sd, 'b3': jax.random.normal(ks[8], (E, F, R), jnp.float32) * 0.01, 'a2': jax.random.normal(ks[9], (E, R, F), jnp.float32) * sf, 'b2': jax.random.normal(ks[10], (E, D, R), jnp.float32) * 0.01}
    _L0_ffn_all = _L0_ffn_setup()
    _L0_ffn_in = {k: v for k, v in _L0_ffn_all.items() if k in ('gate_w', 'w1', 'w3', 'w2', 'a1', 'b1', 'a3', 'b3', 'a2', 'b2')}
    del _L0_ffn_all

    def _L1_xattn_setup():
        import jax, jax.numpy as jnp
        import numpy as np
        D_MODEL = 256
        NUM_HEADS = 16
        HEAD_DIM = D_MODEL // NUM_HEADS

        def _fq_sym(x, axis):
            s = jnp.max(jnp.abs(x), axis=axis, keepdims=True) / 127.0
            s = jnp.maximum(s, 1e-08)
            q = jnp.clip(jnp.round(x / s), -127.0, 127.0) * s
            return x + jax.lax.stop_gradient(q - x)

        def _fq_unsigned(x, axis):
            s = jnp.max(x, axis=axis, keepdims=True) / 255.0
            s = jnp.maximum(s, 1e-08)
            q = jnp.clip(jnp.round(x / s), 0.0, 255.0) * s
            return x + jax.lax.stop_gradient(q - x)
        key = jax.random.key(seed)
        ks = jax.random.split(key, 8)
        B, N, M, C = (2, 256, 64, D_MODEL)
        return {'x': jax.random.normal(ks[0], (B, N, C), jnp.float32), 'cond': jax.random.normal(ks[1], (B, M, C), jnp.float32), 'Wq': jax.random.normal(ks[2], (C, C), jnp.float32) * 0.02, 'bq': jnp.zeros((C,), jnp.float32), 'Wkv': jax.random.normal(ks[3], (C, 2 * C), jnp.float32) * 0.02, 'bkv': jnp.zeros((2 * C,), jnp.float32), 'Wp': jax.random.normal(ks[4], (C, C), jnp.float32) * 0.02, 'bp': jnp.zeros((C,), jnp.float32)}
    _L1_xattn_all = _L1_xattn_setup()
    _L1_xattn_in = {k: v for k, v in _L1_xattn_all.items() if k in ('Wq', 'bq', 'Wkv', 'bkv', 'Wp', 'bp')}
    del _L1_xattn_all

    def _L1_ffn_setup():
        import jax, jax.numpy as jnp
        import numpy as np
        EPS = 1e-05
        RMS_EPS = 1e-06

        def activation_quant(x, num_bits=8):
            qn = -2 ** (num_bits - 1)
            qp = 2 ** (num_bits - 1) - 1
            xf = x.astype(jnp.float32)
            s = qp / jnp.clip(jnp.max(jnp.abs(xf), axis=-1, keepdims=True), EPS, None)
            return (jnp.clip(jnp.round(xf * s), qn, qp) / s).astype(x.dtype)

        def weight_quant(w):
            wf = w.astype(jnp.float32)
            s = 1.0 / jnp.clip(jnp.mean(jnp.abs(wf)), EPS, None)
            return (jnp.clip(jnp.round(wf * s), -1.0, 1.0) / s).astype(w.dtype)

        def bit_linear(x, w):
            qx = x + jax.lax.stop_gradient(activation_quant(x) - x)
            qw = w + jax.lax.stop_gradient(weight_quant(w) - w)
            return jnp.einsum('bsh,oh->bso', qx, qw)

        def rms_norm(x, weight, eps=RMS_EPS):
            xf = x.astype(jnp.float32)
            var = jnp.mean(xf * xf, axis=-1, keepdims=True)
            return weight * (xf * jax.lax.rsqrt(var + eps)).astype(x.dtype)
        key = jax.random.key(seed)
        k1, k2, k3, k4 = jax.random.split(key, 4)
        B, S, H, I = (2, 256, 256, 1024)
        scale = 1.0 / np.sqrt(H)
        return {'x': jax.random.normal(k1, (B, S, H), dtype=jnp.float32), 'w_gate': jax.random.normal(k2, (I, H), dtype=jnp.float32) * scale, 'w_up': jax.random.normal(k3, (I, H), dtype=jnp.float32) * scale, 'w_down': jax.random.normal(k4, (H, I), dtype=jnp.float32) * (1.0 / np.sqrt(I)), 'ln_weight': jnp.ones((I,), dtype=jnp.float32)}
    _L1_ffn_all = _L1_ffn_setup()
    _L1_ffn_in = {k: v for k, v in _L1_ffn_all.items() if k in ('w_gate', 'w_up', 'w_down', 'ln_weight')}
    del _L1_ffn_all
    return {'x': x, 'ctx_2048': ctx_2048, 'mask_BxS2_ik0': mask_BxS2_ik0, 'L0_xattn_Wq': _L0_xattn_in['Wq'], 'L0_xattn_bq': _L0_xattn_in['bq'], 'L0_xattn_Wk': _L0_xattn_in['Wk'], 'L0_xattn_bk': _L0_xattn_in['bk'], 'L0_xattn_Wv': _L0_xattn_in['Wv'], 'L0_xattn_bv': _L0_xattn_in['bv'], 'L0_xattn_Wo': _L0_xattn_in['Wo'], 'L0_xattn_bo': _L0_xattn_in['bo'], 'L0_xattn_ln_gamma': _L0_xattn_in['ln_gamma'], 'L0_xattn_ln_beta': _L0_xattn_in['ln_beta'], 'L0_xattn_residual_scale': _L0_xattn_in['residual_scale'], 'L0_ffn_gate_w': _L0_ffn_in['gate_w'], 'L0_ffn_w1': _L0_ffn_in['w1'], 'L0_ffn_w3': _L0_ffn_in['w3'], 'L0_ffn_w2': _L0_ffn_in['w2'], 'L0_ffn_a1': _L0_ffn_in['a1'], 'L0_ffn_b1': _L0_ffn_in['b1'], 'L0_ffn_a3': _L0_ffn_in['a3'], 'L0_ffn_b3': _L0_ffn_in['b3'], 'L0_ffn_a2': _L0_ffn_in['a2'], 'L0_ffn_b2': _L0_ffn_in['b2'], 'L1_xattn_Wq': _L1_xattn_in['Wq'], 'L1_xattn_bq': _L1_xattn_in['bq'], 'L1_xattn_Wkv': _L1_xattn_in['Wkv'], 'L1_xattn_bkv': _L1_xattn_in['bkv'], 'L1_xattn_Wp': _L1_xattn_in['Wp'], 'L1_xattn_bp': _L1_xattn_in['bp'], 'L1_ffn_w_gate': _L1_ffn_in['w_gate'], 'L1_ffn_w_up': _L1_ffn_in['w_up'], 'L1_ffn_w_down': _L1_ffn_in['w_down'], 'L1_ffn_ln_weight': _L1_ffn_in['ln_weight']}

def reference(x, ctx_2048, mask_BxS2_ik0, L0_xattn_Wq, L0_xattn_bq, L0_xattn_Wk, L0_xattn_bk, L0_xattn_Wv, L0_xattn_bv, L0_xattn_Wo, L0_xattn_bo, L0_xattn_ln_gamma, L0_xattn_ln_beta, L0_xattn_residual_scale, L0_ffn_gate_w, L0_ffn_w1, L0_ffn_w3, L0_ffn_w2, L0_ffn_a1, L0_ffn_b1, L0_ffn_a3, L0_ffn_b3, L0_ffn_a2, L0_ffn_b2, L1_xattn_Wq, L1_xattn_bq, L1_xattn_Wkv, L1_xattn_bkv, L1_xattn_Wp, L1_xattn_bp, L1_ffn_w_gate, L1_ffn_w_up, L1_ffn_w_down, L1_ffn_ln_weight):
    import jax
    import jax.numpy as jnp

    def _L0_xattn_ref(hidden_states, audio_tokens, attention_mask, Wq, bq, Wk, bk, Wv, bv, Wo, bo, ln_gamma, ln_beta, residual_scale):
        import jax, jax.numpy as jnp
        import numpy as np
        import math
        H = 256
        NH = 16
        HD = H // NH
        EPS_LN = 1e-05
        RES_SCALE_MAX = 0.3

        def _nan_clean(x, lim=10000.0):
            return jnp.nan_to_num(x, nan=0.0, posinf=lim, neginf=-lim)
        B, S, _ = hidden_states.shape
        T = audio_tokens.shape[1]
        hs = _nan_clean(hidden_states).astype(jnp.float32)
        at = _nan_clean(audio_tokens).astype(jnp.float32)

        def proj(x, W, b, L):
            y = x @ W.T + b
            return y.reshape(B, L, NH, HD).transpose(0, 2, 1, 3)
        q = _nan_clean(proj(hs, Wq, bq, S))
        k = _nan_clean(proj(at, Wk, bk, T))
        v = _nan_clean(proj(at, Wv, bv, T))
        scale = max(math.sqrt(HD), 1e-08)
        scores = jnp.einsum('bhsd,bhtd->bhst', q, k) / scale
        scores = jnp.clip(scores, -50.0, 50.0)
        scores = jnp.nan_to_num(scores, nan=0.0, posinf=50.0, neginf=-50.0)
        attend = (attention_mask.astype(jnp.float32) > 0.5)[:, None, None, :]
        scores = jnp.where(attend, scores, -10000.0)
        scores = jnp.clip(scores, -50.0, 50.0)
        probs = jax.nn.softmax(scores, axis=-1)
        probs = jnp.nan_to_num(probs, nan=0.0, posinf=1.0, neginf=0.0)
        probs = probs / (probs.sum(axis=-1, keepdims=True) + 1e-08)
        ctx = jnp.einsum('bhst,bhtd->bhsd', probs, v)
        ctx = ctx.transpose(0, 2, 1, 3).reshape(B, S, H)
        delta = _nan_clean(ctx @ Wo.T + bo)
        rs = jnp.clip(residual_scale, 0.0, RES_SCALE_MAX)
        delta = rs * delta
        mu = delta.mean(axis=-1, keepdims=True)
        var = jnp.mean((delta - mu) ** 2, axis=-1, keepdims=True)
        delta = (delta - mu) / jnp.sqrt(var + EPS_LN) * ln_gamma + ln_beta
        return delta

    def _L0_ffn_ref(x, gate_w, w1, w3, w2, a1, b1, a3, b3, a2, b2):
        import jax, jax.numpy as jnp
        import numpy as np
        TOP_K = 2
        LORA_SCALE = 32.0 / 16.0
        B, S, D = x.shape
        E = gate_w.shape[0]
        xf = x.reshape(B * S, D)
        N = xf.shape[0]
        logits = xf @ gate_w.T
        top_w, top_i = jax.lax.top_k(logits, TOP_K)
        routing = jax.nn.softmax(top_w, axis=-1)
        w_full = jnp.zeros((N, E), x.dtype).at[jnp.arange(N)[:, None], top_i].add(routing)
        base1 = xf @ w1.T
        base3 = xf @ w3.T

        def expert_step(acc, p):
            A1, B1, A3, B3, A2, B2, we = p
            h1 = base1 + xf @ A1.T @ B1.T * LORA_SCALE
            h3 = base3 + xf @ A3.T @ B3.T * LORA_SCALE
            act = jax.nn.silu(h1) * h3
            out = act @ w2.T + act @ A2.T @ B2.T * LORA_SCALE
            return (acc + we[:, None] * out, None)
        init = jnp.zeros((N, D), x.dtype)
        out, _ = jax.lax.scan(expert_step, init, (a1, b1, a3, b3, a2, b2, w_full.T))
        return out.reshape(B, S, D)

    def _L1_xattn_ref(x, cond, Wq, bq, Wkv, bkv, Wp, bp):
        import jax, jax.numpy as jnp
        import numpy as np
        D_MODEL = 256
        NUM_HEADS = 16
        HEAD_DIM = D_MODEL // NUM_HEADS

        def _fq_sym(x, axis):
            s = jnp.max(jnp.abs(x), axis=axis, keepdims=True) / 127.0
            s = jnp.maximum(s, 1e-08)
            q = jnp.clip(jnp.round(x / s), -127.0, 127.0) * s
            return x + jax.lax.stop_gradient(q - x)

        def _fq_unsigned(x, axis):
            s = jnp.max(x, axis=axis, keepdims=True) / 255.0
            s = jnp.maximum(s, 1e-08)
            q = jnp.clip(jnp.round(x / s), 0.0, 255.0) * s
            return x + jax.lax.stop_gradient(q - x)
        B, N, C = x.shape
        H, hd = (NUM_HEADS, HEAD_DIM)
        q = (x @ Wq + bq).reshape(1, B * N, H, hd)
        kv = (cond @ Wkv + bkv).reshape(1, -1, 2, H, hd)
        k, v = (kv[:, :, 0], kv[:, :, 1])
        scale = 1.0 / np.sqrt(hd).astype(np.float32)
        q = jnp.transpose(q * scale, (0, 2, 1, 3))
        k = jnp.transpose(k, (0, 2, 1, 3))
        v = jnp.transpose(v, (0, 2, 1, 3))
        q = _fq_sym(q, axis=-1)
        k = _fq_sym(k, axis=-1)
        v = _fq_sym(v, axis=2)
        attn = jnp.einsum('bhqd,bhkd->bhqk', q, k)
        attn = jax.nn.softmax(attn.astype(jnp.float32), axis=-1)
        attn = _fq_unsigned(attn, axis=-1)
        out = jnp.einsum('bhqk,bhkd->bhqd', attn, v)
        out = jnp.transpose(out, (0, 2, 1, 3)).reshape(B, N, C)
        return out @ Wp + bp

    def _L1_ffn_ref(x, w_gate, w_up, w_down, ln_weight):
        import jax, jax.numpy as jnp
        import numpy as np
        EPS = 1e-05
        RMS_EPS = 1e-06

        def activation_quant(x, num_bits=8):
            qn = -2 ** (num_bits - 1)
            qp = 2 ** (num_bits - 1) - 1
            xf = x.astype(jnp.float32)
            s = qp / jnp.clip(jnp.max(jnp.abs(xf), axis=-1, keepdims=True), EPS, None)
            return (jnp.clip(jnp.round(xf * s), qn, qp) / s).astype(x.dtype)

        def weight_quant(w):
            wf = w.astype(jnp.float32)
            s = 1.0 / jnp.clip(jnp.mean(jnp.abs(wf)), EPS, None)
            return (jnp.clip(jnp.round(wf * s), -1.0, 1.0) / s).astype(w.dtype)

        def bit_linear(x, w):
            qx = x + jax.lax.stop_gradient(activation_quant(x) - x)
            qw = w + jax.lax.stop_gradient(weight_quant(w) - w)
            return jnp.einsum('bsh,oh->bso', qx, qw)

        def rms_norm(x, weight, eps=RMS_EPS):
            xf = x.astype(jnp.float32)
            var = jnp.mean(xf * xf, axis=-1, keepdims=True)
            return weight * (xf * jax.lax.rsqrt(var + eps)).astype(x.dtype)
        h = jax.nn.silu(bit_linear(x, w_gate)) * bit_linear(x, w_up)
        h = rms_norm(h, ln_weight)
        return bit_linear(h, w_down)
    x = x + _L0_xattn_ref(_layernorm(x, axis=-1), ctx_2048, mask_BxS2_ik0, L0_xattn_Wq, L0_xattn_bq, L0_xattn_Wk, L0_xattn_bk, L0_xattn_Wv, L0_xattn_bv, L0_xattn_Wo, L0_xattn_bo, L0_xattn_ln_gamma, L0_xattn_ln_beta, L0_xattn_residual_scale)
    x = x + _L0_ffn_ref(_layernorm(x, axis=-1), L0_ffn_gate_w, L0_ffn_w1, L0_ffn_w3, L0_ffn_w2, L0_ffn_a1, L0_ffn_b1, L0_ffn_a3, L0_ffn_b3, L0_ffn_a2, L0_ffn_b2)
    x = x + _L1_xattn_ref(_layernorm(x, axis=-1), ctx_2048, L1_xattn_Wq, L1_xattn_bq, L1_xattn_Wkv, L1_xattn_bkv, L1_xattn_Wp, L1_xattn_bp)
    x = x + _L1_ffn_ref(_layernorm(x, axis=-1), L1_ffn_w_gate, L1_ffn_w_up, L1_ffn_w_down, L1_ffn_ln_weight)
    return x

_drawn_inputs = setup_inputs


def setup_inputs(seed=0):
    import zlib

    import numpy as np

    out = dict(_drawn_inputs(seed))
    spreads = {'L0_xattn_bq': (0.0, 0.1),
     'L0_xattn_bk': (0.0, 0.8),
     'L0_xattn_bv': (0.0, 0.1),
     'L0_xattn_bo': (0.0, 0.1),
     'L0_xattn_ln_gamma': (1.0, 0.2),
     'L0_xattn_ln_beta': (0.0, 0.1),
     'L1_xattn_bq': (0.0, 0.8),
     'L1_xattn_bkv': (0.0, 0.318),
     'L1_xattn_bp': (0.0, 0.1),
     'L1_ffn_ln_weight': (1.0, 0.2)}
    factors = {'L1_xattn_Wq': 8.0, 'L1_xattn_Wkv': 2.854}
    for name, (base, spread) in spreads.items():
        noise = np.random.default_rng([zlib.crc32(name.encode()), seed]).standard_normal(out[name].shape)
        drawn = base * np.exp(spread * noise) if base else spread * noise
        out[name] = jnp.asarray(drawn.astype(out[name].dtype))
    for name, factor in factors.items():
        out[name] = (out[name] * factor).astype(out[name].dtype)
    return out
```

```python
from contextlib import ExitStack

import concourse.bass as bass
from concourse import mybir

F32 = mybir.dt.float32
BF16 = mybir.dt.bfloat16
U16 = mybir.dt.uint16
U32 = mybir.dt.uint32
I32 = mybir.dt.int32
ALU = mybir.AluOpType
ACT = mybir.ActivationFunctionType
AX = mybir.AxisListType

P = 128
N_TOK, D = 1024, 256
BATCH = 256
KD = D // P
TILES = N_TOK // P
H, HD = 16, 16
E, R = 8, 16
NLD = 15
F0 = 704
FH = F0 // 2
FC = 6
FL = F0 - (FC - 1) * P
F1 = 1024
KT = N_TOK // P
MAGIC = 12582912.0
E50 = 5.184705528587072e21
EM50 = 1.9287498479639178e-22
LN255 = 5.541263545158426
LORA = 2.0

CONSTS = ["ident", "headmask", "iota8"]


def build(nc, a, out):
    ctx = ExitStack()

    def sb(name, shape, dt=F32):
        return ctx.enter_context(nc.sbuf_tensor(name, shape, dt))

    def bank(name, shape, dt=F32):
        return ctx.enter_context(nc.psum_tensor(name, shape, dt))

    sems = {}

    class Sems:
        def __getitem__(self, name):
            if name not in sems:
                sems[name] = ctx.enter_context(nc.semaphore(name))
            return sems[name]

    S = Sems()

    with ctx:
        ident = sb("ident_s", [P, P])
        identb = sb("identb", [P, P], BF16)
        headmask = sb("headmask_s", [P, 8])
        iota8 = sb("iota8_s", [P, E])
        ones = sb("ones", [P, P])
        wq0 = sb("wq0_s", [P, KD, D])
        wk0 = sb("wk0_s", [P, KD, D])
        wv0 = sb("wv0_s", [P, KD, D])
        wo0 = sb("wo0_s", [P, KD, D])
        wq1 = sb("wq1_s", [P, KD, D])
        wkv1 = sb("wkv1_s", [P, KD, 2 * D])
        wp1 = sb("wp1_s", [P, KD, D])
        a13g = sb("a13g_s", [P, KD, 2 * P + E])
        w13 = sb("w13_s", [P, KD, 2 * F0])
        b13 = sb("b13_s", [P, 2 * F0])
        w2a2 = sb("w2a2_s", [P, FC, D + P])
        b2 = sb("b2_s", [P, D])
        colb = sb("colb_s", [P, 3, KD])
        rowb = sb("rowb_s", [P, 7, D])
        lnw = sb("lnw_s", [P, F1])
        rs = sb("rs_s", [P, 1])
        maski = sb("maski_s", [P, 8], I32)
        ehi = sb("ehi", [P, 8])
        wraw = sb("wraw", [P, 3, 2048])
        tern = sb("tern", [P, 3, 2048], BF16)
        asum = sb("asum", [P, 3])
        wsc = sb("wsc", [P, 3])
        wrs = sb("wrs", [P, 3])
        eps5 = sb("eps5", [P, 1])
        mhalf = sb("mhalf", [P, 1])
        BV0, BO0, GAM, BET, BQ1, BK1, BP1 = range(7)

        ctxt = sb("ctxt", [P, 2, KD, P])
        k0all = sb("k0all", [P, KD, N_TOK])
        v0all = sb("v0all", [P, TILES, H, HD + 1])
        v1t = sb("v1t", [P, KD, N_TOK])
        v1qf = sb("v1qf", [P, N_TOK])
        v1q = v1qf[:, :].bitcast(BF16).rearrange("p (k n) -> p k n", k=KD)
        v1i = sb("v1i", [P, KT, D], BF16)
        k1t = sb("k1t", [P, 8, N_TOK], BF16)
        kf = sb("kf", [P, D])
        kam = sb("kam", [P, H])
        krs = sb("krs", [P, H])
        kr1 = sb("kr1", [P, D])
        kst = sb("kst", [P, H, 4, HD], BF16)
        vam = sb("vam", [P, KD])
        vsc = sb("vsc", [P, KD])
        vrs = sb("vrs", [P, KD])

        xin = sb("xin", [P, 2, D])
        st6 = sb("st6", [P, 6])
        mv = sb("mv", [P, 2])
        ve = sb("ve", [P, 1])
        spare = sb("spare", [P, 1])
        rstd = sb("rstd", [P, 1])
        xn = sb("xn", [P, D])
        xT = sb("xT", [P, KD, P])
        qbd = wraw[:, 2, :].rearrange("p (m h q) -> p m h q", m=KD, h=8)
        kcur = sb("kcur", [P, KD, BATCH])
        vcur = sb("vcur", [P, 2, H, HD + 1])
        e0 = wraw[:, 0:2, :].rearrange("p k (h q) -> p k h q", h=H)
        den0 = sb("den0", [P, H])
        ctx0 = sb("ctx0", [P, H, HD])
        cT = sb("cT", [P, KD, P])
        bors = sb("bors", [P, D])
        xb = sb("xb", [P, D])
        dl = sb("dl", [P, D])
        x1 = sb("x1", [P, D])
        lg = sb("lg", [P, E])
        top = sb("top", [P, 8])
        topi = sb("topi", [P, 8], U32)
        topf = sb("topf", [P, 2])
        oh = sb("oh", [P, 2, E])
        dm = sb("dm", [P, 1])
        em = sb("em", [P, 1])
        em1 = sb("em1", [P, 1])
        rw = sb("rw", [P, 2])
        us = sb("us", [P, 2, 2, E, R])
        usT = sb("usT", [P, 4, P])
        th = sb("th", [P, FH])
        gs = sb("gs", [P, FH])
        aw = sb("aw", [P, 2, F0])
        awT = sb("awT", [P, 2, FC, P])
        gT = sb("gT", [P, FC, P])
        zz = sb("zz", [P, 2, P])
        zm = sb("zm", [P, P])
        zT = sb("zT", [P, P])
        x2 = sb("x2", [P, D])

        bst6 = sb("bst6", [P, 6])
        bmv = sb("bmv", [P, 2])
        bve = sb("bve", [P, 1])
        brstd = sb("brstd", [P, 1])
        bxn = sb("bxn", [P, D])
        x2b = sb("x2b", [P, D])
        bxT = sb("bxT", [P, KD, P])
        qf = sb("qf", [P, D])
        qam = sb("qam", [P, H])
        qsc = sb("qsc", [P, H])
        nqsc = sb("nqsc", [P, H])
        qrs = sb("qrs", [P, H])
        qst = sb("qst", [P, H, 4, HD], BF16)
        qiT = sb("qiT", [P, 8, P], BF16)
        mx = sb("mx", [P, H])
        nb = sb("nb", [P, H])
        nq = sb("nq", [P, 2, N_TOK], U16)
        nT = sb("nT", [P, 2, KT, P], BF16)
        wabs = nT[:, :, :, :].rearrange("p a k q -> p (a k q)")
        s255 = sb("s255", [P, H])
        r255 = sb("r255", [P, H])
        o1 = wv0[:, 0, :].rearrange("p (h d) -> p h d", h=H)
        oT = wv0[:, 1, :].rearrange("p (k q) -> p k q", k=KD)
        x3 = wk0[:, 1, :]
        xam = sb("xam", [P, 1])
        xrs = sb("xrs", [P, 1])
        xs = sb("xs", [P, 1])
        xi = sb("xi", [P, D], BF16)
        xiT = sb("xiT", [P, KD, P], BF16)
        al = sb("al", [P, 3])
        bth = v1t[:, 0, :]
        hg = v1t[:, 1, :]
        hr = v1qf
        sq = sb("sq", [P, 8])
        hi = wkv1[:, 0, :].bitcast(BF16)
        hiT = wkv1[:, 1, :].bitcast(BF16).rearrange("p (k q) -> p k q", k=8)
        yo = wk0[:, 0, :]

        fA = bank("fA", [P, 512])
        fB = bank("fB", [P, 512])
        s0 = bank("s0", [P, 1024])
        s1 = bank("s1", [P, 1024])
        SB_ = [s0, s1]
        tb = bank("tb", [P, 8, P], BF16)
        ob = bank("ob", [P, 512])
        NA = NB = 13
        NT = 19
        NO = 6
        NS = 9

        def evac_nT(eng, copy, t, h):
            eng.wait_ge(S["p_t"], NT * t + h + 2)
            if h >= 2:
                eng.wait_ge(S["p_pv"], H * t + h - 1)
            copy(nT[:, h % 2, :, :], tb[:, :, :].bitcast(U16)).then_inc(S["tb_free"], 1)

        block = ctx.enter_context(nc.Block())

        @block.sync
        def _(sp):
            def load(dst, src, name):
                sp.dma_start(dst, src).then_inc(S[name], 16)

            load(wkv1[:, :, :], a["wkv1"], "ld_wctx")
            load(wk0[:, :, :], a["wk0"], "ld_wctx")
            load(wv0[:, :, :], a["wv0"], "ld_wctx")
            load(colb[:, :, :], a["colb"], "ld_wctx")
            load(ident[:, :], a["ident"], "ld_wctx")
            load(headmask[:, :], a["headmask"], "ld_wctx")
            load(iota8[:, :], a["iota8"], "ld_wctx")
            load(maski[:, :], a["maski"], "ld_wctx")
            for i, n in enumerate(["bv0", "bo0", "gamma", "beta", "bq1", "bk1", "bp1"]):
                load(rowb[:, i, :], a[n].partition_broadcast(P), "ld_wctx")
            load(rs[:, :], a["rs"].partition_broadcast(P), "stored")
            for s in range(2):
                load(ctxt[:, s, :, :], a["ctxt"][s], "ld_ctx%d" % s)
            with sp.Fori(1, TILES // 2) as u:
                for s in range(2):
                    sp.wait_ge(S["pk1"], 2 * u + s - 1)
                    load(ctxt[:, s, :, :], a["ctxt"][bass.ds(2 * u + s, 1)].rearrange("a p k t -> (a p) k t"),
                         "ld_ctx%d" % s)
            for n, dst in (("wq0", wq0), ("wo0", wo0), ("a13g", a13g), ("w13", w13), ("b13", b13),
                           ("w2a2", w2a2), ("b2", b2), ("wq1", wq1), ("wp1", wp1), ("lnw", lnw)):
                src = a[n].partition_broadcast(P) if n == "lnw" else a[n]
                load(dst[tuple(slice(None) for _ in dst.shape)], src, "ld_w")
            load(xin[:, 0, :], a["x"][0:P, :], "ld_x")
            with sp.Fori(1, TILES) as t:
                sp.wait_ge(S["xin_free"], t)
                load(xin[:, 0, :], a["x"][bass.ts(t, P), :], "ld_x")
                sp.wait_ge(S["yo_ready"], t)
                sp.dma_start(out[bass.ts(t - 1, P), :], yo[:, :]).then_inc(S["stored"], 16)
            sp.wait_ge(S["yo_ready"], TILES)
            sp.dma_start(out[(TILES - 1) * P:TILES * P, :], yo[:, :]).then_inc(S["stored"], 16)
            sp.wait_ge(S["stored"], 16 * (TILES + 1))

        @block.gpsimd
        def _(pool):
            for i, n in enumerate(("wg1", "wu1", "wd1")):
                pool.dma_start(wraw[:, i, :], a[n]).then_inc(S["ld_tern"], 16)
            pool.memset(ones[:, :], 1.0).then_inc(S["consts"], 1)
            pool.memset(eps5[:, :], 1e-5).then_inc(S["consts"], 1)
            pool.memset(mhalf[:, :], -0.5).then_inc(S["consts"], 1)
            pool.memset(kst[:, :, 3, :], 0.0).then_inc(S["consts"], 1)
            pool.memset(qst[:, :, 3, :], 0.0).then_inc(S["consts"], 1)
            pool.memset(v0all[:, :, :, HD:HD + 1], 1.0).then_inc(S["consts"], 1)

            def rsqrt(var_ready, ve_, rstd_, name, t):
                pool.wait_ge(S[var_ready], t + 1)
                pool.tensor_tensor(rstd_[:, :], ve_[:, :], mhalf[:, :], ALU.pow).then_inc(S[name], 1)

            pool.wait_ge(S["consts"], 6)
            pool.wait_ge(S["k0_done"], TILES * 2)
            pool.wait_ge(S["v0_done"], TILES)
            with pool.Fori(0, TILES) as t:
                b = (t // 2) * BATCH
                pool.tensor_copy(kcur[:, :, :], k0all[:, :, bass.ds(b, BATCH)]).then_inc(S["kv_ready"], 1)
                pool.tensor_copy(vcur[:, :, :, :], v0all[:, bass.ds((t // 2) * 2, 2), :, :]).then_inc(S["kv_ready"], 1)
                rsqrt("var1", ve, rstd, "rstd1", t)
                pool.wait_ge(S["ld_x"], 16 * t + 16)
                pool.tensor_tensor(xb[:, :], xin[:, 0, :], rowb[:, BET, :], ALU.add).then_inc(S["xb_ready"], 1)
                rsqrt("var2", ve, rstd, "rstd2", t)
                rsqrt("var3", ve, rstd, "rstd3", t)
                pool.wait_ge(S["awT_ready"], 4 * t + 4)
                pool.tensor_tensor(gT[:, 0:FC - 1, :], awT[:, 0, 0:FC - 1, :], awT[:, 1, 0:FC - 1, :],
                                   ALU.add).then_inc(S["gT_ready"], 1)
                pool.tensor_tensor(gT[0:FL, FC - 1, :], awT[0:FL, 0, FC - 1, :], awT[0:FL, 1, FC - 1, :],
                                   ALU.add).then_inc(S["gT_ready"], 1)
                pool.wait_ge(S["x2_ready"], t + 1)
                pool.tensor_tensor(x2b[:, :], x2[:, :], rowb[:, BP1, :], ALU.add).then_inc(S["x2b_ready"], 1)
                rsqrt("var4", bve, brstd, "rstd4", t)
                rsqrt("var5", bve, brstd, "rstd5", t)
                rsqrt("var6", bve, brstd, "rstd6", t)

        @block.scalar
        def _(act):
            act.wait_ge(S["ld_wctx"], 16 * NLD)

            with act.Fori(0, TILES) as t:
                act.wait_ge(S["pk0"], t + 1)
                for m in range(KD):
                    act.activation(k0all[:, m, bass.ds(t * P, P)], fA[:, m * P:(m + 1) * P], ACT.Identity,
                                   bias=colb[:, 1, m:m + 1]).then_inc(S["k0_done"], 1)
                act.wait_ge(S["pv1"], t + 1)
                for m in range(KD):
                    act.activation(v1t[:, m, bass.ds(t * P, P)], fB[:, m * P:(m + 1) * P], ACT.Identity,
                                   bias=colb[:, 2, m:m + 1]).then_inc(S["v1t_done"], 1)
                act.wait_ge(S["pk1T"], t + 1)
                act.activation(k1t[:, :, bass.ds(t * P, P)], tb[:, :, :], ACT.Copy).then_inc(S["k1T_done"], 1)
            for i in range(3):
                act.wait_ge(S["ld_tern"], 48)
                if i:
                    act.wait_ge(S["asum"], i)
                act.activation(wabs[:, :], wraw[:, i, :], ACT.Abs, accum_out=asum[:, i:i + 1]).then_inc(S["asum"], 1)
            for m in range(KD):
                act.wait_ge(S["pv1iT"], m + 1)
                act.activation(v1i[:, :, m * P:(m + 1) * P], tb[:, :, :], ACT.Copy).then_inc(S["v1i_done"], 1)

            def copy_out(dst, src, full, ready, t, free):
                act.wait_ge(S[full], t + 1)
                act.activation(dst, src, ACT.Copy).then_inc(S[ready], 1)

            with act.Fori(0, TILES) as t:
                copy_out(xT[:, :, :], fA[:, 0:D], "p_xT1", "xT1", t, None)
                for j in range(8):
                    m, half, kt = j // 4, (j // 2) % 2, j % 2
                    bk = (fA, fB)[j % 2]
                    act.wait_ge(S["p_sc"], 8 * t + j + 1)
                    h4 = 8 * m + 4 * half
                    act.activation(e0[:, kt, h4:h4 + 4, :], bk[:, 0:512], ACT.Exp).then_inc(S["e0"], 1)
                copy_out(cT[:, :, :], fB[:, 0:D], "p_cT", "cT", t, None)
                copy_out(xT[:, :, :], fB[:, 0:D], "p_xT2", "xT2", t, None)
                act.wait_ge(S["dmax"], t + 1)
                act.activation(em[:, :], dm[:, :], ACT.Exp).then_inc(S["em"], 1)
                copy_out(usT[:, :, :], fB[:, 0:512], "p_usT", "usT", t, None)
                for j in range(2):
                    for s in range(2):
                        act.wait_ge(S["p_h1"], 4 * t + 2 * j + s + 1)
                        if j + s:
                            act.wait_ge(S["gs"], 4 * t + 2 * j + s)
                        act.activation(th[:, :], fA[:, 0:FH], ACT.Tanh, scale=0.5).then_inc(S["th"], 1)
                for s in range(2):
                    act.wait_ge(S["p_awT"], 3 * t + s + 1)
                    act.activation(awT[:, s, 0:4, :], (fA, fB)[s][:, 0:512], ACT.Copy).then_inc(S["awT_ready"], 1)
                act.wait_ge(S["p_awT"], 3 * t + 3)
                act.activation(awT[:, :, 4, :], fA[:, 0:256], ACT.Copy).then_inc(S["awT_ready"], 1)
                act.activation(awT[0:FL, :, 5, :], fA[0:FL, 256:512], ACT.Copy).then_inc(S["awT_ready"], 1)
                copy_out(zT[:, :], fA[:, 0:P], "p_zT", "zT", t, None)
                copy_out(bxT[:, :, :], ob[:, 0:D], "p_xT3", "bxT", t, None)
                act.wait_ge(S["p_t"], NT * t + 1)
                act.activation(qiT[:, :, :], tb[:, :, :], ACT.Copy).then_inc(S["tb_free"], 1)
                for h in range(H):
                    act.wait_ge(S["nb"], H * t + h + 1)
                    if h >= 2:
                        act.wait_ge(S["p_t"], NT * t + h)
                    act.activation(nq[:, h % 2, :], SB_[h % 2][:, :], ACT.Exp, scale=qsc[:, h:h + 1],
                                   bias=nb[:, h:h + 1], accum_out=s255[:, h:h + 1]).then_inc(S["nq"], 1)
                    if h % 2 == 0 and h >= 1:
                        evac_nT(act, act.copy, t, h - 1)
                evac_nT(act, act.copy, t, H - 1)
                act.wait_ge(S["p_oT"], t + 1)
                for m in range(KD):
                    act.activation(oT[:, m, :], ob[:, m * P:(m + 1) * P], ACT.Copy,
                                   scale=vsc[:, m:m + 1]).then_inc(S["oT"], 1)
                act.wait_ge(S["p_t"], NT * t + 18)
                act.activation(xiT[:, :, :], tb[:, 0:KD, :], ACT.Copy).then_inc(S["tb_free"], 1)
                act.wait_ge(S["p_g"], t + 1)
                act.wait_ge(S["al"], t + 1)
                act.activation(bth[:, :], s0[:, :], ACT.Tanh, scale=al[:, 1:2]).then_inc(S["bth"], 1)
                act.wait_ge(S["p_t"], NT * t + 19)
                act.activation(hiT[:, :, :], tb[:, :, :], ACT.Copy).then_inc(S["tb_free"], 1)

        @block.vector
        def _(dve):
            v = nc.vector
            n = [0]
            PRO = [0, 0]

            def link(ins, t=None, apart=False):
                n[0] += 1
                if t is None:
                    ins.then_inc(S["dve_pro"], 1)
                    dve.wait_ge(S["dve_pro"], n[0])
                else:
                    sem, size = t[1], t[2]
                    ins.then_inc(S[sem], 1)
                    dve.wait_ge(S[sem], t[0] * size + n[0])
                    if apart:
                        v.memset(spare[:, :], 0.0)

            dve.wait_ge(S["ld_wctx"], 16 * NLD)
            v.tensor_copy(identb[:, :], ident[:, :]).then_inc(S["identb"], 1)
            dve.wait_ge(S["stored"], 16)
            link(v.tensor_scalar(rs[:, :], rs[:, :], 0.0, 0.3, ALU.max, ALU.min))
            link(v.tensor_scalar(bors[:, :], rowb[:, BO0, :], rs[:, 0:1], None, ALU.mult))
            link(v.tensor_copy(ehi[:, :], maski[:, :]))
            link(v.tensor_scalar(ehi[:, :], ehi[:, :], 0.5, None, ALU.is_gt))
            link(v.tensor_scalar(ehi[:, :], ehi[:, :], E50, EM50, ALU.mult, ALU.add))
            link(v.tensor_scalar(rowb[:, BQ1, :], rowb[:, BQ1, :], 0.25, None, ALU.mult))
            dve.wait_ge(S["consts"], 6)
            base = n[0]
            n[0] = 0
            CH = 9
            with dve.Fori(0, TILES) as t:
                T = (t, "dve_ctx", CH)
                n[0] = 0
                dve.wait_ge(S["pv0"], t + 1)
                v.tensor_tensor(v0all[:, bass.ds(t, 1), :, 0:HD], ob[:, 0:D].rearrange("p (a h d) -> p a h d", a=1, d=HD),
                                rowb[:, BV0, :].rearrange("p (a h d) -> p a h d", a=1, d=HD),
                                ALU.add).then_inc(S["v0_done"], 1)
                dve.wait_ge(S["pk1"], t + 1)
                link(v.tensor_tensor(kf[:, :], s0[:, 0:D], rowb[:, BK1, :], ALU.add), T)
                kf3 = kf[:, :].rearrange("p (h d) -> p h d", d=HD)
                kr3 = kr1[:, :].rearrange("p (h d) -> p h d", d=HD)
                link(v.tensor_reduce(kam[:, :], kf3, AX.X, ALU.max, apply_absolute_value=True), T)
                link(v.tensor_scalar(kam[:, :], kam[:, :], 1.0 / 127.0, 1e-8, ALU.mult, ALU.max), T)
                link(v.reciprocal(krs[:, :], kam[:, :]), T)
                link(v.tensor_tensor(kf3, kf3, krs[:, :].unsqueeze(2).to_broadcast([P, H, HD]), ALU.mult), T)
                link(v.tensor_scalar(kf[:, :], kf[:, :], MAGIC, MAGIC, ALU.add, ALU.subtract), T)
                link(v.tensor_tensor(kf3, kf3, kam[:, :].unsqueeze(2).to_broadcast([P, H, HD]), ALU.mult), T)
                v.tensor_copy(kst[:, :, 0, :], kf3).then_inc(S["kst_part"], 1)
                dve.wait_ge(S["kst_part"], 3 * t + 1)
                link(v.tensor_tensor(kr3, kf3, kst[:, :, 0, :], ALU.subtract), T)
                v.tensor_copy(kst[:, :, 1, :], kr3).then_inc(S["kst_part"], 1)
                dve.wait_ge(S["kst_part"], 3 * t + 2)
                link(v.tensor_tensor(kr3, kr3, kst[:, :, 1, :], ALU.subtract), T)
                v.tensor_copy(kst[:, :, 2, :], kr3).then_inc(S["kst_part"], 1)
                assert n[0] == CH
            n[0] = base

            dve.wait_ge(S["v1t_done"], 2 * TILES)
            link(v.tensor_reduce(vam[:, :], v1t[:, :, :], AX.X, ALU.max, apply_absolute_value=True))
            link(v.tensor_scalar(vsc[:, :], vam[:, :], 1.0 / 127.0, 1e-8, ALU.mult, ALU.max))
            link(v.reciprocal(vrs[:, :], vsc[:, :]))
            for m in range(KD):
                link(v.tensor_scalar(v1t[:, m, :], v1t[:, m, :], vrs[:, m:m + 1], MAGIC, ALU.mult, ALU.add))
                v.tensor_scalar(v1q[:, m, :], v1t[:, m, :], MAGIC, None, ALU.subtract).then_inc(S["v1q"], 1)
            dve.wait_ge(S["p_asum"], 1)
            link(v.tensor_scalar(wsc[:, :], ob[:, 0:3], 1.0 / (F1 * D), 1e-5, ALU.mult, ALU.max))
            link(v.reciprocal(wrs[:, :], wsc[:, :]))
            for i in range(3):
                link(v.tensor_scalar(wraw[:, i, :], wraw[:, i, :], wrs[:, i:i + 1], 1.0, ALU.mult, ALU.min))
                link(v.tensor_scalar(wraw[:, i, :], wraw[:, i, :], -1.0, MAGIC, ALU.max, ALU.add))
                v.tensor_scalar(tern[:, i, :], wraw[:, i, :], MAGIC, None, ALU.subtract).then_inc(S["tern"], 1)

            def layernorm(src, stats, mean_var, var_eps, rstd_, dst, var_name, rstd_name, T, ready):
                t = T[0]
                link(v.bn_stats(stats[:, :], src), T, apart=True)
                link(v.bn_aggr(mean_var[:, :], stats[:, :]), T)
                v.tensor_scalar(var_eps[:, :], mean_var[:, 1:2], 1e-5, None, ALU.add).then_inc(S[var_name], 1)
                dve.wait_ge(S[rstd_name], t + 1)
                if dst is not None:
                    v.tensor_scalar(dst[:, :], src, mean_var[:, 0:1], rstd_[:, 0:1], ALU.subtract,
                                    ALU.mult).then_inc(S[ready], 1)

            FR, BK = FR_LINKS, BK_LINKS
            with dve.Fori(0, TILES) as t:
                T = (t, "dve_front", FR)
                n[0] = 0
                dve.wait_ge(S["ld_x"], 16 * t + 16)
                layernorm(xin[:, 0, :], st6, mv, ve, rstd, xn, "var1", "rstd1", T, "xn1")
                dve.wait_ge(S["p_qT"], t + 1)
                for m in range(KD):
                    v.scalar_tensor_tensor(
                        qbd[:, m, :, :], fB[:, m * P:(m + 1) * P].unsqueeze(1).to_broadcast([P, 8, P]),
                        colb[:, 0, m:m + 1], headmask[:, :].unsqueeze(2).to_broadcast([P, 8, P]),
                        ALU.add, ALU.mult).then_inc(S["qbd"], 1)
                for j in range(8):
                    m, half, kt = j // 4, (j // 2) % 2, j % 2
                    h4 = 8 * m + 4 * half
                    dve.wait_ge(S["e0"], 8 * t + j + 1)
                    v.tensor_scalar(e0[:, kt, h4:h4 + 4, :], e0[:, kt, h4:h4 + 4, :],
                                        ehi[:, bass.ds((t // 2) * 2 + kt, 1)], EM50, ALU.min,
                                        ALU.max).then_inc(S["e0c"], 1)
                dve.wait_ge(S["p_ctx"], t + 1)
                c3 = fA[:, 0:H * (HD + 1)].rearrange("p (h d) -> p h d", d=HD + 1)
                link(v.reciprocal(den0[:, :], c3[:, :, HD]), T)
                v.tensor_tensor(ctx0[:, :, :], c3[:, :, 0:HD], den0[:, :].unsqueeze(2).to_broadcast([P, H, HD]),
                                ALU.mult).then_inc(S["ctx0"], 1)
                dve.wait_ge(S["p_dl"], t + 1)
                v.scalar_tensor_tensor(dl[:, :], fA[:, 0:D], rs[:, 0:1], bors[:, :], ALU.mult,
                                       ALU.add).then_inc(S["dl"], 1)
                dve.wait_ge(S["dl"], t + 1)
                layernorm(dl[:, :], st6, mv, ve, rstd, None, "var2", "rstd2", T, None)
                link(v.scalar_tensor_tensor(dl[:, :], dl[:, :], mv[:, 0:1], rowb[:, GAM, :], ALU.subtract,
                                            ALU.mult), T)
                dve.wait_ge(S["xb_ready"], t + 1)
                v.scalar_tensor_tensor(x1[:, :], dl[:, :], rstd[:, 0:1], xb[:, :], ALU.mult,
                                       ALU.add).then_inc(S["xin_free"], 1)
                dve.wait_ge(S["xin_free"], t + 1)
                layernorm(x1[:, :], st6, mv, ve, rstd, xn, "var3", "rstd3", T, "xn2")
                dve.wait_ge(S["p_ul"], t + 1)
                link(v.tensor_copy(lg[:, :], fA[:, 2 * P:2 * P + E]), T, apart=True)
                link(v.max(top[:, :], lg[:, :]), T)
                v.tensor_tensor(dm[:, :], top[:, 1:2], top[:, 0:1], ALU.subtract).then_inc(S["dmax"], 1)
                link(v.max_index(topi[:, :], top[:, :], lg[:, :]), T)
                link(v.tensor_copy(topf[:, :], topi[:, 0:2]), T)
                for s in range(2):
                    link(v.tensor_scalar(oh[:, s, :], iota8[:, :], topf[:, s:s + 1], LORA, ALU.is_equal,
                                         ALU.mult), T)
                u4 = fA[:, 0:2 * P].rearrange("p (a e r) -> p a e r", a=2, e=E)
                for s in range(2):
                    link(v.tensor_tensor(us[:, s, :, :, :], u4,
                                         oh[:, s, :].unsqueeze(1).unsqueeze(3).to_broadcast([P, 2, E, R]),
                                         ALU.mult), T)
                v.tensor_tensor(us[:, 1, :, :, :], us[:, 1, :, :, :], us[:, 0, :, :, :],
                                ALU.subtract).then_inc(S["us"], 1)
                dve.wait_ge(S["em"], t + 1)
                link(v.tensor_scalar(em1[:, :], em[:, :], 1.0, None, ALU.add), T)
                link(v.reciprocal(rw[:, 0:1], em1[:, :]), T)
                link(v.tensor_tensor(rw[:, 1:2], rw[:, 0:1], em[:, :], ALU.mult), T)
                link(v.tensor_scalar(rw[:, :], rw[:, :], 0.5, None, ALU.mult), T)
                for j in range(2):
                    for s in range(2):
                        dve.wait_ge(S["th"], 4 * t + 2 * j + s + 1)
                        if j + s:
                            dve.wait_ge(S["aw"], 4 * t + 2 * j + s)
                        v.scalar_tensor_tensor(gs[:, :], th[:, :], 1.0, fA[:, 0:FH], ALU.add,
                                               ALU.mult).then_inc(S["gs"], 1)
                        dve.wait_ge(S["gs"], 4 * t + 2 * j + s + 1)
                        dve.wait_ge(S["p_h3"], 4 * t + 2 * j + s + 1)
                        v.scalar_tensor_tensor(aw[:, s, j * FH:(j + 1) * FH], gs[:, :], rw[:, s:s + 1],
                                               fB[:, 0:FH], ALU.mult, ALU.mult).then_inc(S["aw"], 1)
                dve.wait_ge(S["p_z"], t + 1)
                link(v.tensor_tensor(zz[:, :, :].rearrange("p s (e r) -> p (s e) r", r=R),
                                     fB[:, 0:2 * P].rearrange("p (e r) -> p e r", r=R),
                                     oh[:, :, :].rearrange("p s e -> p (s e)").unsqueeze(2).to_broadcast([P, 2 * E, R]),
                                     ALU.mult), T)
                v.tensor_tensor(zm[:, :], zz[:, 0, :], zz[:, 1, :], ALU.add).then_inc(S["zm"], 1)
                dve.wait_ge(S["p_y"], t + 1)
                v.tensor_tensor(x2[:, :], fB[:, 0:D], x1[:, :], ALU.add).then_inc(S["x2_ready"], 1)
                dve.wait_ge(S["x2_ready"], t + 1)
                assert n[0] == FR, ("FR", n[0])

                T = (t, "dve_back", BK)
                n[0] = 0
                layernorm(x2[:, :], bst6, bmv, bve, brstd, bxn, "var4", "rstd4", T, "xn3")
                dve.wait_ge(S["p_q1"], t + 1)
                v.scalar_tensor_tensor(qf[:, :], ob[:, 0:D], 0.25, rowb[:, BQ1, :], ALU.mult,
                                       ALU.add).then_inc(S["qf"], 1)
                dve.wait_ge(S["qf"], t + 1)
                qf3 = qf[:, :].rearrange("p (h d) -> p h d", d=HD)
                link(v.tensor_reduce(qam[:, :], qf3, AX.X, ALU.max, apply_absolute_value=True), T)
                link(v.tensor_scalar(qsc[:, :], qam[:, :], 1.0 / 127.0, 1e-8, ALU.mult, ALU.max), T)
                link(v.tensor_scalar(nqsc[:, :], qsc[:, :], -1.0, None, ALU.mult), T)
                link(v.reciprocal(qrs[:, :], qsc[:, :]), T)
                link(v.tensor_tensor(qf3, qf3, qrs[:, :].unsqueeze(2).to_broadcast([P, H, HD]), ALU.mult), T)
                v.tensor_scalar(qst[:, :, 0:3, :], qf3.unsqueeze(2).to_broadcast([P, H, 3, HD]), MAGIC, MAGIC,
                                ALU.add, ALU.subtract).then_inc(S["qst"], 1)
                for h in range(H):
                    dve.wait_ge(S["p_s"], H * t + h + 1)
                    v.tensor_reduce(mx[:, h:h + 1], SB_[h % 2][:, :], AX.X, ALU.max).then_inc(S["mx"], 1)
                    dve.wait_ge(S["mx"], H * t + h + 1)
                    v.tensor_scalar(nb[:, h:h + 1], mx[:, h:h + 1], nqsc[:, h:h + 1], LN255, ALU.mult,
                                    ALU.add).then_inc(S["nb"], 1)
                    if h % 2 and h >= 1:
                        evac_nT(dve, v.tensor_copy, t, h - 1)
                dve.wait_ge(S["nq"], H * t + H)
                link(v.reciprocal(r255[:, :], s255[:, :]), T)
                dve.wait_ge(S["p_pv"], H * t + H)
                v.tensor_tensor(o1[:, :, :], ob[:, 0:D].rearrange("p (h d) -> p h d", d=HD),
                                r255[:, :].unsqueeze(2).to_broadcast([P, H, HD]), ALU.mult).then_inc(S["o1"], 1)
                dve.wait_ge(S["p_d2"], t + 1)
                dve.wait_ge(S["x2b_ready"], t + 1)
                v.tensor_tensor(x3[:, :], ob[:, 0:D], x2b[:, :], ALU.add).then_inc(S["x3"], 1)
                dve.wait_ge(S["x3"], t + 1)
                layernorm(x3[:, :], bst6, bmv, bve, brstd, bxn, "var5", "rstd5", T, "xn4")
                dve.wait_ge(S["xn4"], t + 1)
                link(v.tensor_reduce(xam[:, :], bxn[:, :], AX.X, ALU.max, apply_absolute_value=True), T)
                link(v.tensor_scalar(xam[:, :], xam[:, :], 1e-5, 1.0 / 127.0, ALU.max, ALU.mult), T)
                link(v.reciprocal(xrs[:, :], xam[:, :]), T)
                link(v.tensor_scalar(bxn[:, :], bxn[:, :], xrs[:, 0:1], MAGIC, ALU.mult, ALU.add), T)
                v.tensor_scalar(xi[:, :], bxn[:, :], MAGIC, None, ALU.subtract).then_inc(S["xi"], 1)
                link(v.tensor_tensor(al[:, 0:1], xam[:, :], wsc[:, 0:1], ALU.mult), T)
                link(v.tensor_tensor(al[:, 2:3], xam[:, :], wsc[:, 1:2], ALU.mult), T)
                v.tensor_scalar(al[:, 1:2], al[:, 0:1], 0.5, None, ALU.mult).then_inc(S["al"], 1)
                dve.wait_ge(S["al"], t + 1)
                link(v.tensor_tensor(sq[:, 0:1], al[:, 1:2], al[:, 2:3], ALU.mult), T)
                dve.wait_ge(S["bth"], t + 1)
                link(v.scalar_tensor_tensor(hg[:, :], bth[:, :], 1.0, s0[:, :], ALU.add, ALU.mult), T)
                dve.wait_ge(S["p_u"], t + 1)
                v.tensor_tensor(hg[:, :], hg[:, :], s1[:, :], ALU.mult).then_inc(S["hg"], 1)
                dve.wait_ge(S["hg"], t + 1)
                link(v.scalar_tensor_tensor(bth[:, :], hg[:, :], 1.0, hg[:, :], ALU.mult, ALU.mult,
                                            accum_out=sq[:, 1:2]), T)
                link(v.tensor_tensor(sq[:, 2:3], sq[:, 0:1], sq[:, 0:1], ALU.mult), T)
                link(v.tensor_tensor(sq[:, 2:3], sq[:, 2:3], sq[:, 1:2], ALU.mult), T)
                v.tensor_scalar(bve[:, :], sq[:, 2:3], 1.0 / F1, 1e-6, ALU.mult, ALU.add).then_inc(S["var6"], 1)
                link(v.tensor_tensor(hr[:, :], hg[:, :], lnw[:, :], ALU.mult), T)
                link(v.tensor_reduce(sq[:, 3:4], hr[:, :], AX.X, ALU.max, apply_absolute_value=True), T)
                dve.wait_ge(S["rstd6"], t + 1)
                link(v.tensor_tensor(sq[:, 4:5], brstd[:, :], sq[:, 0:1], ALU.mult), T)
                link(v.tensor_tensor(sq[:, 5:6], sq[:, 3:4], sq[:, 4:5], ALU.mult), T)
                link(v.tensor_scalar(sq[:, 5:6], sq[:, 5:6], 1e-5, 1.0 / 127.0, ALU.max, ALU.mult), T)
                link(v.reciprocal(sq[:, 6:7], sq[:, 5:6]), T)
                link(v.tensor_tensor(sq[:, 6:7], sq[:, 6:7], sq[:, 4:5], ALU.mult), T)
                link(v.tensor_scalar(hr[:, :], hr[:, :], sq[:, 6:7], MAGIC, ALU.mult, ALU.add), T)
                v.tensor_scalar(hi[:, :], hr[:, :], MAGIC, None, ALU.subtract).then_inc(S["hi"], 1)
                link(v.tensor_tensor(sq[:, 7:8], sq[:, 5:6], wsc[:, 2:3], ALU.mult), T)
                dve.wait_ge(S["p_y1"], t + 1)
                dve.wait_ge(S["stored"], 16 * t + 16)
                v.scalar_tensor_tensor(yo[:, :], ob[:, 0:D], sq[:, 7:8], x3[:, :], ALU.mult,
                                       ALU.add).then_inc(S["yo_ready"], 1)
                assert n[0] == BK, ("BK", n[0])

        @block.tensor
        def _(pe):
            mm = nc.tensor.matmul
            tr = nc.tensor.transpose

            def proj(outs, lhs, rhs):
                for k in range(KD):
                    i = mm(outs, lhs(k), rhs(k), start=(k == 0), stop=(k == KD - 1))
                return i

            pe.wait_ge(S["ld_wctx"], 16 * NLD)
            pe.wait_ge(S["identb"], 1)
            pe.wait_ge(S["consts"], 6)
            with pe.Fori(0, TILES // 2) as u:
                for s in range(2):
                    pe.wait_ge(S["ld_ctx%d" % s], 16 * u + 16)
                    c = ctxt[:, s]
                    tt = 2 * u + s
                    for m in range(KD):
                        i = proj(fA[:, m * P:(m + 1) * P], lambda k: wk0[:, k, m * P:(m + 1) * P], lambda k: c[:, k, :])
                    i.then_inc(S["pk0"], 1)
                    for m in range(KD):
                        i = proj(fB[:, m * P:(m + 1) * P], lambda k: wkv1[:, k, D + m * P:D + (m + 1) * P], lambda k: c[:, k, :])
                    i.then_inc(S["pv1"], 1)
                    proj(ob[:, 0:D], lambda k: c[:, k, :], lambda k: wv0[:, k, :]).then_inc(S["pv0"], 1)
                    proj(s0[:, 0:D], lambda k: c[:, k, :], lambda k: wkv1[:, k, 0:D]).then_inc(S["pk1"], 1)
                    pe.wait_ge(S["kst_part"], 3 * tt + 3)
                    for g in range(8):
                        i = tr(tb[:, g, :], kst[:, 2 * g:2 * g + 2, :, :].rearrange("p a b c -> p (a b c)"), identb[:, :])
                    i.then_inc(S["pk1T"], 1)
                    pe.wait_ge(S["k0_done"], 2 * tt + 2)
                    pe.wait_ge(S["v1t_done"], 2 * tt + 2)
                    pe.wait_ge(S["v0_done"], tt + 1)
                    pe.wait_ge(S["k1T_done"], tt + 1)
            pe.wait_ge(S["asum"], 3)
            pe.wait_ge(S["v0_done"], TILES)
            mm(ob[:, 0:3], ones[:, :], asum[:, :], start=True, stop=True).then_inc(S["p_asum"], 1)
            for m in range(KD):
                pe.wait_ge(S["v1q"], m + 1)
                if m:
                    pe.wait_ge(S["v1i_done"], m)
                else:
                    pe.wait_ge(S["k1T_done"], TILES)
                for k in range(KT):
                    i = tr(tb[:, k, :], v1q[:, m, k * P:(k + 1) * P], identb[:, :])
                i.then_inc(S["pv1iT"], 1)
            pe.wait_ge(S["v1i_done"], KD)
            pe.wait_ge(S["tern"], 3)
            pe.wait_ge(S["ld_w"], 16 * 10)

            wl = [P] * (FC - 1) + [FL]
            with pe.Fori(0, TILES) as t:
                def turn(bk, src, ready, full):
                    pe.wait_ge(S[ready], t + 1)
                    for k in range(KD):
                        i = tr(bk[:, k * P:(k + 1) * P], src[:, k * P:(k + 1) * P], ident[:, :])
                    i.then_inc(S[full], 1)

                turn(fA, xn, "xn1", "p_xT1")
                pe.wait_ge(S["xT1"], t + 1)
                for m in range(KD):
                    i = proj(fB[:, m * P:(m + 1) * P], lambda k: wq0[:, k, m * P:(m + 1) * P], lambda k: xT[:, k, :])
                i.then_inc(S["p_qT"], 1)
                pe.wait_ge(S["kv_ready"], 2 * t + 2)
                pe.wait_ge(S["qbd"], 2 * t + 2)
                for j in range(8):
                    m, half, kt = j // 4, (j // 2) % 2, j % 2
                    if j >= 2:
                        pe.wait_ge(S["e0"], 8 * t + j - 1)
                    mm((fA, fB)[j % 2][:, 0:512], kcur[:, m, kt * P:(kt + 1) * P],
                       qbd[:, m, 4 * half:4 * half + 4, :], start=True, stop=True).then_inc(S["p_sc"], 1)
                pe.wait_ge(S["e0c"], 8 * t + 8)
                for h in range(H):
                    for kt in range(2):
                        i = mm(fA[:, h * (HD + 1):(h + 1) * (HD + 1)], e0[:, kt, h, :], vcur[:, kt, h, :],
                               start=(kt == 0), stop=(kt == 1))
                i.then_inc(S["p_ctx"], 1)
                turn(fB, ctx0[:, :, :].rearrange("p h d -> p (h d)"), "ctx0", "p_cT")
                pe.wait_ge(S["cT"], t + 1)
                proj(fA[:, 0:D], lambda k: cT[:, k, :], lambda k: wo0[:, k, :]).then_inc(S["p_dl"], 1)
                turn(fB, xn, "xn2", "p_xT2")
                pe.wait_ge(S["xT2"], t + 1)
                proj(fA[:, 0:2 * P + E], lambda k: xT[:, k, :], lambda k: a13g[:, k, :]).then_inc(S["p_ul"], 1)
                pe.wait_ge(S["us"], t + 1)
                for s in range(2):
                    for q in range(2):
                        i = tr(fB[:, (2 * s + q) * P:(2 * s + q + 1) * P],
                               us[:, s, q, :, :].rearrange("p e r -> p (e r)"), ident[:, :])
                i.then_inc(S["p_usT"], 1)
                pe.wait_ge(S["usT"], t + 1)
                for j in range(2):
                    for q in range(2):
                        bk, col = (fA, fB)[q], q * F0 + j * FH
                        if j:
                            pe.wait_ge(S["aw"], 4 * t + 2)
                        for k in range(KD):
                            mm(bk[:, 0:FH], xT[:, k, :], w13[:, k, col:col + FH], start=(k == 0), stop=False,
                               skip_group_check=True)
                        mm(bk[:, 0:FH], usT[:, q, :], b13[:, col:col + FH], start=False, stop=False,
                           skip_group_check=True).then_inc(S[("p_h1", "p_h3")[q]], 1)
                    for q in range(2):
                        bk, col = (fA, fB)[q], q * F0 + j * FH
                        pe.wait_ge(S[("gs", "aw")[q]], 4 * t + 2 * j + 1)
                        mm(bk[:, 0:FH], usT[:, 2 + q, :], b13[:, col:col + FH], start=False, stop=True,
                           skip_group_check=True).then_inc(S[("p_h1", "p_h3")[q]], 1)
                pe.wait_ge(S["aw"], 4 * t + 4)
                for s in range(2):
                    for c in range(4):
                        i = tr((fA, fB)[s][:, c * P:(c + 1) * P], aw[:, s, c * P:(c + 1) * P], ident[:, :])
                    i.then_inc(S["p_awT"], 1)
                pe.wait_ge(S["awT_ready"], 4 * t + 1)
                for c in (4, 5):
                    for s in range(2):
                        w = wl[c]
                        i = tr(fA[0:w, ((c - 4) * 2 + s) * P:((c - 4) * 2 + s + 1) * P],
                               aw[:, s, c * P:c * P + w], ident[:, :])
                i.then_inc(S["p_awT"], 1)
                pe.wait_ge(S["awT_ready"], 4 * t + 4)
                for s in range(2):
                    for c in range(FC):
                        i = mm(fB[:, s * P:(s + 1) * P], awT[0:wl[c], s, c, :], w2a2[0:wl[c], c, D:D + P],
                               start=(c == 0), stop=(c == FC - 1))
                i.then_inc(S["p_z"], 1)
                pe.wait_ge(S["zm"], t + 1)
                tr(fA[:, 0:P], zm[:, :], ident[:, :]).then_inc(S["p_zT"], 1)
                pe.wait_ge(S["gT_ready"], 2 * t + 2)
                for c in range(FC):
                    mm(fB[:, 0:D], gT[0:wl[c], c, :], w2a2[0:wl[c], c, 0:D], start=(c == 0), stop=False)
                pe.wait_ge(S["zT"], t + 1)
                mm(fB[:, 0:D], zT[:, :], b2[:, :], start=False, stop=True).then_inc(S["p_y"], 1)

                turn(ob, bxn, "xn3", "p_xT3")
                pe.wait_ge(S["bxT"], t + 1)
                proj(ob[:, 0:D], lambda k: bxT[:, k, :], lambda k: wq1[:, k, :]).then_inc(S["p_q1"], 1)
                pe.wait_ge(S["qst"], t + 1)
                for g in range(8):
                    i = tr(tb[:, g, :], qst[:, 2 * g:2 * g + 2, :, :].rearrange("p a b c -> p (a b c)"), identb[:, :])
                i.then_inc(S["p_t"], 1)
                pe.wait_ge(S["tb_free"], NT * t + 1)

                def scores(h):
                    if h >= 2:
                        pe.wait_ge(S["nq"], H * t + h - 1)
                    lo = 64 * (h % 2)
                    for c in range(2):
                        i = mm(SB_[h % 2][:, c * 512:(c + 1) * 512], qiT[lo:lo + 64, h // 2, :],
                               k1t[lo:lo + 64, h // 2, c * 512:(c + 1) * 512], start=True, stop=True)
                    i.then_inc(S["p_s"], 1)

                def turn_n(h):
                    pe.wait_ge(S["nq"], H * t + h + 1)
                    pe.wait_ge(S["tb_free"], NT * t + h + 1)
                    src = nq[:, h % 2, :].bitcast(BF16)
                    for k in range(KT):
                        i = tr(tb[:, k, :], src[:, k * P:(k + 1) * P], identb[:, :])
                    i.then_inc(S["p_t"], 1)

                def weigh(h):
                    pe.wait_ge(S["tb_free"], NT * t + h + 2)
                    for k in range(KT):
                        i = mm(ob[:, h * HD:(h + 1) * HD], nT[:, h % 2, k, :], v1i[:, k, h * HD:(h + 1) * HD],
                               start=(k == 0), stop=(k == KT - 1))
                    i.then_inc(S["p_pv"], 1)

                pe.wait_ge(S["qf"], t + 1)
                scores(0)
                scores(1)
                for h in range(H):
                    turn_n(h)
                    if h + 2 < H:
                        scores(h + 2)
                    if h:
                        weigh(h - 1)
                weigh(H - 1)
                turn(ob, o1[:, :, :].rearrange("p h d -> p (h d)"), "o1", "p_oT")
                pe.wait_ge(S["oT"], 2 * t + 2)
                proj(ob[:, 0:D], lambda k: oT[:, k, :], lambda k: wp1[:, k, :]).then_inc(S["p_d2"], 1)
                pe.wait_ge(S["xi"], t + 1)
                for k in range(KD):
                    i = tr(tb[:, k, :], xi[:, k * P:(k + 1) * P], identb[:, :])
                i.then_inc(S["p_t"], 1)
                pe.wait_ge(S["tb_free"], NT * t + 18)
                for g in range(2):
                    for c in range(2):
                        for k in range(KD):
                            i = mm(SB_[g][:, c * 512:(c + 1) * 512], xiT[:, k, :],
                                   tern[:, g, k * F1 + c * 512:k * F1 + (c + 1) * 512],
                                   start=(k == 0), stop=(k == KD - 1))
                    i.then_inc(S[("p_g", "p_u")[g]], 1)
                pe.wait_ge(S["hi"], t + 1)
                for k in range(8):
                    i = tr(tb[:, k, :], hi[:, k * P:(k + 1) * P], identb[:, :])
                i.then_inc(S["p_t"], 1)
                pe.wait_ge(S["tb_free"], NT * t + 19)
                for k in range(8):
                    i = mm(ob[:, 0:D], hiT[:, k, :], tern[:, 2, k * D:(k + 1) * D], start=(k == 0), stop=(k == 7))
                i.then_inc(S["p_y1"], 1)


FR_LINKS = 21
BK_LINKS = 30


def lay_out(inputs):
    import numpy as np
    g = {k: np.asarray(v) for k, v in inputs.items()}

    def rows(w):
        return np.ascontiguousarray(w.reshape(-1, P, w.shape[1]).transpose(1, 0, 2))

    er = lambda w: w.reshape(E * R, -1)
    w2a2 = np.zeros((FC * P, D + P), np.float32)
    w2a2[:F0, :D] = g["L0_ffn_w2"].T
    w2a2[:F0, D:] = er(g["L0_ffn_a2"]).T
    col = lambda b: b.reshape(KD, P).T
    kv = g["L1_xattn_bkv"]
    hm = np.zeros((P, 8), np.float32)
    hm[np.arange(P), np.arange(P) // HD] = float(HD) ** -0.5
    arrays = {
        "x": g["x"].reshape(N_TOK, D),
        "ctxt": g["ctx_2048"].reshape(TILES, P, KD, P).transpose(0, 3, 2, 1),
        "ident": np.eye(P, dtype=np.float32),
        "headmask": hm,
        "iota8": np.tile(np.arange(E, dtype=np.float32), (P, 1)),
        "maski": g["mask_BxS2_ik0"].reshape(8, P).T,
        "wq0": rows(g["L0_xattn_Wq"].T), "wk0": rows(g["L0_xattn_Wk"].T),
        "wv0": rows(g["L0_xattn_Wv"].T), "wo0": rows(g["L0_xattn_Wo"].T),
        "wq1": rows(g["L1_xattn_Wq"]), "wkv1": rows(g["L1_xattn_Wkv"]), "wp1": rows(g["L1_xattn_Wp"]),
        "a13g": rows(np.concatenate([er(g["L0_ffn_a1"]).T, er(g["L0_ffn_a3"]).T, g["L0_ffn_gate_w"].T], 1)),
        "w13": rows(np.concatenate([g["L0_ffn_w1"].T, g["L0_ffn_w3"].T], 1)),
        "b13": np.concatenate([er(g["L0_ffn_b1"].transpose(0, 2, 1)), er(g["L0_ffn_b3"].transpose(0, 2, 1))], 1),
        "w2a2": rows(w2a2),
        "b2": er(g["L0_ffn_b2"].transpose(0, 2, 1)),
        "colb": np.stack([col(g["L0_xattn_bq"]), col(g["L0_xattn_bk"]), col(kv[D:])], 1),
        "bv0": g["L0_xattn_bv"], "bo0": g["L0_xattn_bo"], "gamma": g["L0_xattn_ln_gamma"],
        "beta": g["L0_xattn_ln_beta"], "bq1": g["L1_xattn_bq"], "bk1": kv[:D], "bp1": g["L1_xattn_bp"],
        "rs": g["L0_xattn_residual_scale"].reshape(1),
        "lnw": g["L1_ffn_ln_weight"],
        "wg1": rows(g["L1_ffn_w_gate"].T).reshape(P, -1), "wu1": rows(g["L1_ffn_w_up"].T).reshape(P, -1),
        "wd1": rows(g["L1_ffn_w_down"].T).reshape(P, -1),
    }
    return {k: np.ascontiguousarray(v) for k, v in arrays.items()}


def kernel(**inputs):
    import concourse.bacc as _bacc
    from concourse.bass_utils import run_bass_kernel_spmd as _run

    arrays = lay_out(inputs)
    nc = _bacc.Bacc("TRN2", target_bir_lowering=False, num_devices=1)
    aps = {k: nc.dram_tensor("in_" + k, v.shape, mybir.dt.from_np(v.dtype), kind="ExternalInput").ap()
           for k, v in arrays.items()}
    out = nc.dram_tensor("out_y", (N_TOK, D), F32, kind="ExternalOutput").ap()
    build(nc, aps, out)
    r = _run(nc, [{"in_" + k: v for k, v in arrays.items()}], core_ids=[0])
    return r.results[0]["out_y"].reshape(4, BATCH, D)
```

```python
from contextlib import ExitStack

import concourse.bass as bass
from concourse import mybir

F32 = mybir.dt.float32
BF16 = mybir.dt.bfloat16
U16 = mybir.dt.uint16
U32 = mybir.dt.uint32
I32 = mybir.dt.int32
ALU = mybir.AluOpType
ACT = mybir.ActivationFunctionType
AX = mybir.AxisListType

P = 128
N_TOK, D = 1024, 256
BATCH = 256
KD = D // P
TILES = N_TOK // P
H, HD = 16, 16
E, R = 8, 16
NLD = 15
F0 = 704
FH = F0 // 2
FC = 6
FL = F0 - (FC - 1) * P
F1 = 1024
KT = N_TOK // P
MAGIC = 12582912.0
E50 = 5.184705528587072e21
EM50 = 1.9287498479639178e-22
LN255 = 5.541263545158426
LORA = 2.0


def build(nc, a, out):
    ctx = ExitStack()

    def sb(name, shape, dt=F32):
        return ctx.enter_context(nc.sbuf_tensor(name, shape, dt))

    def bank(name, shape, dt=F32):
        return ctx.enter_context(nc.psum_tensor(name, shape, dt))

    sems = {}

    class Sems:
        def __getitem__(self, name):
            if name not in sems:
                sems[name] = ctx.enter_context(nc.semaphore(name))
            return sems[name]

    S = Sems()

    with ctx:
        ident = sb("ident_s", [P, P])
        identb = sb("identb", [P, P], BF16)
        headmask = sb("headmask_s", [P, 8])
        iota8 = sb("iota8_s", [P, E])
        ones = sb("ones", [P, P])
        wq0 = sb("wq0_s", [P, KD, D])
        wk0 = sb("wk0_s", [P, KD, D])
        wv0 = sb("wv0_s", [P, KD, D])
        wo0 = sb("wo0_s", [P, KD, D])
        wq1 = sb("wq1_s", [P, KD, D])
        wkv1 = sb("wkv1_s", [P, KD, 2 * D])
        wp1 = sb("wp1_s", [P, KD, D])
        a13g = sb("a13g_s", [P, KD, 2 * P + E])
        w13 = sb("w13_s", [P, KD, 2 * F0])
        b13 = sb("b13_s", [P, 2 * F0])
        w2a2 = sb("w2a2_s", [P, FC, D + P])
        b2 = sb("b2_s", [P, D])
        colb = sb("colb_s", [P, 3, KD])
        rowb = sb("rowb_s", [P, 7, D])
        lnw = sb("lnw_s", [P, F1])
        rs = sb("rs_s", [P, 1])
        maski = sb("maski_s", [P, 8], I32)
        ehi = sb("ehi", [P, 8])
        wraw = sb("wraw", [P, 3, 2048])
        tern = sb("tern", [P, 3, 2048], BF16)
        asum = sb("asum", [P, 3])
        wsc = sb("wsc", [P, 3])
        wrs = sb("wrs", [P, 3])
        eps5 = sb("eps5", [P, 1])
        mhalf = sb("mhalf", [P, 1])
        BV0, BO0, GAM, BET, BQ1, BK1, BP1 = range(7)

        ctxt = sb("ctxt", [P, 2, KD, P])
        k0all = sb("k0all", [P, KD, N_TOK])
        v0all = sb("v0all", [P, TILES, H, HD + 1])
        v1t = sb("v1t", [P, KD, N_TOK])
        v1qf = sb("v1qf", [P, N_TOK])
        v1q = v1qf[:, :].bitcast(BF16).rearrange("p (k n) -> p k n", k=KD)
        v1i = sb("v1i", [P, KT, D], BF16)
        k1t = sb("k1t", [P, 8, N_TOK], BF16)
        kf = sb("kf", [P, D])
        kam = sb("kam", [P, H])
        krs = sb("krs", [P, H])
        kr1 = sb("kr1", [P, D])
        kst = sb("kst", [P, H, 4, HD], BF16)
        vam = sb("vam", [P, KD])
        vsc = sb("vsc", [P, KD])
        vrs = sb("vrs", [P, KD])

        xin = sb("xin", [P, 2, D])
        st6 = sb("st6", [P, 6])
        mv = sb("mv", [P, 2])
        ve = sb("ve", [P, 1])
        spare = sb("spare", [P, 1])
        rstd = sb("rstd", [P, 1])
        xn = sb("xn", [P, D])
        xT = sb("xT", [P, KD, P])
        qbd = wraw[:, 2, :].rearrange("p (m h q) -> p m h q", m=KD, h=8)
        kcur = sb("kcur", [P, KD, BATCH])
        vcur = sb("vcur", [P, 2, H, HD + 1])
        e0 = wraw[:, 0:2, :].rearrange("p k (h q) -> p k h q", h=H)
        den0 = sb("den0", [P, H])
        ctx0 = sb("ctx0", [P, H, HD])
        cT = sb("cT", [P, KD, P])
        bors = sb("bors", [P, D])
        xb = sb("xb", [P, D])
        dl = sb("dl", [P, D])
        x1 = sb("x1", [P, D])
        lg = sb("lg", [P, E])
        top = sb("top", [P, 8])
        topi = sb("topi", [P, 8], U32)
        topf = sb("topf", [P, 2])
        oh = sb("oh", [P, 2, E])
        dm = sb("dm", [P, 1])
        em = sb("em", [P, 1])
        em1 = sb("em1", [P, 1])
        rw = sb("rw", [P, 2])
        us = sb("us", [P, 2, 2, E, R])
        usT = sb("usT", [P, 4, P])
        th = sb("th", [P, FH])
        gs = sb("gs", [P, FH])
        aw = sb("aw", [P, 2, F0])
        awT = sb("awT", [P, 2, FC, P])
        gT = sb("gT", [P, FC, P])
        zz = sb("zz", [P, 2, P])
        zm = sb("zm", [P, P])
        zT = sb("zT", [P, P])
        x2 = sb("x2", [P, D])

        bst6 = sb("bst6", [P, 6])
        bmv = sb("bmv", [P, 2])
        bve = sb("bve", [P, 1])
        brstd = sb("brstd", [P, 1])
        bxn = sb("bxn", [P, D])
        x2b = sb("x2b", [P, D])
        bxT = sb("bxT", [P, KD, P])
        qf = sb("qf", [P, D])
        qam = sb("qam", [P, H])
        qsc = sb("qsc", [P, 2, H])
        qrs = sb("qrs", [P, H])
        qst = sb("qst", [P, H, 4, HD], BF16)
        qiT = sb("qiT", [P, 8, P], BF16)
        mx = sb("mx", [P, H])
        nb = sb("nb", [P, H])
        nq = sb("nq", [P, 2, N_TOK], U16)
        nT = sb("nT", [P, 2, KT, P], BF16)
        wabs = nT[:, :, :, :].rearrange("p a k q -> p (a k q)")
        qiT_n = sb("qiT_n", [P, 8, P], BF16)
        qsc_n = sb("qsc_n", [P, 2, H])
        s255 = sb("s255", [P, H])
        r255 = sb("r255", [P, H])
        o1 = wv0[:, 0, :].rearrange("p (h d) -> p h d", h=H)
        oT = wv0[:, 1, :].rearrange("p (k q) -> p k q", k=KD)
        x3 = wk0[:, 1, :]
        xam = sb("xam", [P, 1])
        xrs = sb("xrs", [P, 1])
        xs = sb("xs", [P, 1])
        xi = sb("xi", [P, D], BF16)
        xiT = sb("xiT", [P, KD, P], BF16)
        al = sb("al", [P, 3])
        bth = v1t[:, 0, :]
        hg = v1t[:, 1, :]
        hr = v1qf
        sq = sb("sq", [P, 8])
        hi = wkv1[:, 0, :].bitcast(BF16)
        hiT = wkv1[:, 1, :].bitcast(BF16).rearrange("p (k q) -> p k q", k=8)
        yo = wk0[:, 0, :]

        fA = bank("fA", [P, 512])
        fB = bank("fB", [P, 512])
        s0 = bank("s0", [P, 1024])
        s1 = bank("s1", [P, 1024])
        SB_ = [s0, s1]
        tb = bank("tb", [P, 8, P], BF16)
        ob = bank("ob", [P, 512])

        def run(steps, point, tiles):
            for name in PLAN[point]:
                k = tiles[name[0]]
                if k is not None and name in steps:
                    steps[name](k)

        def sweep(engine, iteration):
            iteration(dict(a=0, b=None, c=None))
            iteration(dict(a=1, b=0, c=None))
            with engine.Fori(2, TILES) as i:
                iteration(dict(a=i, b=i - 1, c=i - 2))
            iteration(dict(a=None, b=TILES - 1, c=TILES - 2))
            iteration(dict(a=None, b=None, c=TILES - 1))

        block = ctx.enter_context(nc.Block())

        @block.sync
        def _(sp):
            def load(dst, src, name):
                sp.dma_start(dst, src).then_inc(S[name], 16)

            load(wkv1[:, :, :], a["wkv1"], "ld_wctx")
            load(wk0[:, :, :], a["wk0"], "ld_wctx")
            load(wv0[:, :, :], a["wv0"], "ld_wctx")
            load(colb[:, :, :], a["colb"], "ld_wctx")
            load(ident[:, :], a["ident"], "ld_wctx")
            load(headmask[:, :], a["headmask"], "ld_wctx")
            load(iota8[:, :], a["iota8"], "ld_wctx")
            load(maski[:, :], a["maski"], "ld_wctx")
            for i, n in enumerate(["bv0", "bo0", "gamma", "beta", "bq1", "bk1", "bp1"]):
                load(rowb[:, i, :], a[n].partition_broadcast(P), "ld_wctx")
            load(rs[:, :], a["rs"].partition_broadcast(P), "stored")
            for s in range(2):
                load(ctxt[:, s, :, :], a["ctxt"][s], "ld_ctx%d" % s)
            with sp.Fori(1, TILES // 2) as u:
                for s in range(2):
                    sp.wait_ge(S["pk1"], 2 * u + s - 1)
                    load(ctxt[:, s, :, :], a["ctxt"][bass.ds(2 * u + s, 1)].rearrange("a p k t -> (a p) k t"),
                         "ld_ctx%d" % s)
            for n, dst in (("wq0", wq0), ("wo0", wo0), ("a13g", a13g), ("w13", w13), ("b13", b13),
                           ("w2a2", w2a2), ("b2", b2), ("wq1", wq1), ("wp1", wp1), ("lnw", lnw)):
                src = a[n].partition_broadcast(P) if n == "lnw" else a[n]
                load(dst[tuple(slice(None) for _ in dst.shape)], src, "ld_w")
            load(xin[:, 0, :], a["x"][0:P, :], "ld_x")
            with sp.Fori(1, TILES) as t:
                sp.wait_ge(S["xin_free"], t)
                load(xin[:, 0, :], a["x"][bass.ts(t, P), :], "ld_x")

        @block.gpsimd
        def _(pool):
            for i, n in enumerate(("wg1", "wu1", "wd1")):
                pool.dma_start(wraw[:, i, :], a[n]).then_inc(S["ld_tern"], 16)
            pool.memset(ones[:, :], 1.0).then_inc(S["consts"], 1)
            pool.memset(eps5[:, :], 1e-5).then_inc(S["consts"], 1)
            pool.memset(mhalf[:, :], -0.5).then_inc(S["consts"], 1)
            pool.memset(kst[:, :, 3, :], 0.0).then_inc(S["consts"], 1)
            pool.memset(qst[:, :, 3, :], 0.0).then_inc(S["consts"], 1)
            pool.memset(v0all[:, :, :, HD:HD + 1], 1.0).then_inc(S["consts"], 1)

            def rsqrt(n, var, to):
                def step(k):
                    pool.wait_ge(S["var%d" % n], k + 1)
                    pool.tensor_tensor(to[:, :], var[:, :], mhalf[:, :], ALU.pow).then_inc(S["rstd%d" % n], 1)
                return step

            def kv(k):
                if ints(k) != 0:
                    pool.wait_ge(S["p_ctx"], k)
                b = (k // 2) * BATCH
                pool.tensor_copy(kcur[:, :, :], k0all[:, :, bass.ds(b, BATCH)]).then_inc(S["kv_ready"], 1)
                pool.tensor_copy(vcur[:, :, :, :], v0all[:, bass.ds((k // 2) * 2, 2), :, :]).then_inc(S["kv_ready"], 1)

            def st1(k):
                rsqrt(1, ve, rstd)(k)
                pool.wait_ge(S["ld_x"], 16 * k + 16)
                pool.tensor_tensor(xb[:, :], xin[:, 0, :], rowb[:, BET, :], ALU.add).then_inc(S["xb_ready"], 1)

            def awt(k):
                pool.wait_ge(S["awT_ready"], 4 * k + 4)
                pool.tensor_tensor(gT[:, 0:FC - 1, :], awT[:, 0, 0:FC - 1, :], awT[:, 1, 0:FC - 1, :],
                                   ALU.add).then_inc(S["gT_ready"], 1)
                pool.tensor_tensor(gT[0:FL, FC - 1, :], awT[0:FL, 0, FC - 1, :], awT[0:FL, 1, FC - 1, :],
                                   ALU.add).then_inc(S["gT_ready"], 1)

            def x2bias(k):
                pool.wait_ge(S["x2_ready"], k + 1)
                if ints(k) != 0:
                    pool.wait_ge(S["x3"], k)
                pool.tensor_tensor(x2b[:, :], x2[:, :], rowb[:, BP1, :], ALU.add).then_inc(S["x2b_ready"], 1)

            steps = {"a_st1": st1, "a_dl": rsqrt(2, ve, rstd), "a_x1": rsqrt(3, ve, rstd), "a_awT": awt,
                     "a_y": rsqrt(4, ve, rstd), "b_x2b": x2bias, "c_d2": rsqrt(5, bve, brstd),
                     "c_rms": rsqrt(6, bve, brstd)}

            pool.wait_ge(S["consts"], 6)
            pool.wait_ge(S["k0_done"], TILES * 2)
            pool.wait_ge(S["v0_done"], TILES)

            def iteration(tiles):
                if tiles["a"] is not None:
                    kv(tiles["a"])
                for point in range(POINTS):
                    run(steps, point, tiles)

            sweep(pool, iteration)

        def evac_nT(eng, copy, b, h):
            eng.wait_ge(S["p_nT"], H * b + h + 1)
            if h >= 2:
                eng.wait_ge(S["p_pv"], H * b + h - 1)
            copy(nT[:, h % 2, :, :], tb[:, :, :].bitcast(U16)).then_inc(S["nT"], 1)

        @block.scalar
        def _(act):
            act.wait_ge(S["ld_wctx"], 16 * NLD)
            act.preload_act_table(ACT.Exp)

            with act.Fori(0, TILES) as t:
                act.wait_ge(S["pk0"], t + 1)
                for m in range(KD):
                    act.activation(k0all[:, m, bass.ds(t * P, P)], fA[:, m * P:(m + 1) * P], ACT.Identity,
                                   bias=colb[:, 1, m:m + 1]).then_inc(S["k0_done"], 1)
                act.wait_ge(S["pv1"], t + 1)
                for m in range(KD):
                    act.activation(v1t[:, m, bass.ds(t * P, P)], fB[:, m * P:(m + 1) * P], ACT.Identity,
                                   bias=colb[:, 2, m:m + 1]).then_inc(S["v1t_done"], 1)
                act.wait_ge(S["pk1T"], t + 1)
                act.activation(k1t[:, :, bass.ds(t * P, P)], tb[:, :, :], ACT.Copy).then_inc(S["k1T_done"], 1)
            act.wait_ge(S["ld_tern"], 48)
            for i in range(3):
                if i:
                    act.wait_ge(S["asum"], i)
                act.activation(wabs[:, :], wraw[:, i, :], ACT.Abs, accum_out=asum[:, i:i + 1]).then_inc(S["asum"], 1)
            for m in range(KD):
                act.wait_ge(S["pv1iT"], m + 1)
                act.activation(v1i[:, :, m * P:(m + 1) * P], tb[:, :, :], ACT.Copy).then_inc(S["v1i_done"], 1)

            def copy_out(dst, src, full, done):
                def step(k):
                    act.wait_ge(S[full], k + 1)
                    act.activation(dst, src, ACT.Copy).then_inc(S[done], 1)
                return step

            def sc(j0):
                def step(k):
                    for j in (j0, j0 + 1):
                        h4, kt = 4 * (j // 2), j % 2
                        act.wait_ge(S["p_sc"], 8 * k + j + 1)
                        act.activation(e0[:, kt, h4:h4 + 4, :], (fA, fB)[j % 2][:, 0:512],
                                       ACT.Exp).then_inc(S["e0"], 1)
                return step

            def ul(k):
                act.wait_ge(S["dmax"], k + 1)
                act.activation(em[:, :], dm[:, :], ACT.Exp).then_inc(S["em"], 1)

            def gate(n):
                def step(k):
                    act.wait_ge(S["p_h1"], 4 * k + n + 1)
                    if n:
                        act.wait_ge(S["gs"], 4 * k + n)
                    act.activation(th[:, :], fA[:, 0:FH], ACT.Tanh, scale=0.5).then_inc(S["th"], 1)
                return step

            def awt(k):
                for s in range(2):
                    act.wait_ge(S["p_awT"], 3 * k + s + 1)
                    act.activation(awT[:, s, 0:4, :], (fA, fB)[s][:, 0:512], ACT.Copy).then_inc(S["awT_ready"], 1)
                act.wait_ge(S["p_awT"], 3 * k + 3)
                act.activation(awT[:, :, 4, :], fA[:, 0:256], ACT.Copy).then_inc(S["awT_ready"], 1)
                act.activation(awT[0:FL, :, 5, :], fA[0:FL, 256:512], ACT.Copy).then_inc(S["awT_ready"], 1)

            def ot(k):
                act.wait_ge(S["p_oT"], k + 1)
                for m in range(KD):
                    act.activation(oT[:, m, :], fB[:, m * P:(m + 1) * P], ACT.Copy,
                                   scale=vsc[:, m:m + 1]).then_inc(S["oT"], 1)

            def gu(k):
                act.wait_ge(S["p_g"], k + 1)
                act.wait_ge(S["al"], k + 1)
                act.activation(bth[:, :], s0[:, :], ACT.Tanh, scale=al[:, 1:2]).then_inc(S["bth"], 1)

            def store(k):
                act.wait_ge(S["yo_ready"], k + 1)
                act.dma_start(out[bass.ts(k, P), :], yo[:, :]).then_inc(S["stored"], 16)

            steps = {"a_xn1": copy_out(xT[:, :, :], fA[:, 0:D], "p_xT1", "xT1"),
                     "a_sc0": sc(0), "a_sc1": sc(2), "a_sc2": sc(4), "a_sc3": sc(6),
                     "a_cT": copy_out(cT[:, :, :], fB[:, 0:D], "p_cT", "cT"),
                     "a_xn2": copy_out(xT[:, :, :], fB[:, 0:D], "p_xT2", "xT2"),
                     "a_ul": ul, "a_us": copy_out(usT[:, :, :], fB[:, 0:512], "p_usT", "usT"),
                     "a_h00": gate(0), "a_h01": gate(1), "a_h10": gate(2), "a_h11": gate(3),
                     "a_awT": awt, "a_y": copy_out(zT[:, :], fA[:, 0:P], "p_zT", "zT"),
                     "a_xn3": copy_out(bxT[:, :, :], fA[:, 0:D], "p_xT3", "bxT"),
                     "a_qiT": copy_out(qiT_n[:, :, :], tb[:, :, :], "p_qiT", "qiT_n"),
                     "c_oT": ot, "c_xiT": copy_out(xiT[:, :, :], tb[:, 0:KD, :], "p_xiT", "xiT"),
                     "c_gu": gu, "c_hiT": copy_out(hiT[:, :, :], tb[:, :, :], "p_hiT", "hiT"),
                     "c_st": store}

            def iteration(tiles):
                b = tiles["b"]
                for h in range(H):
                    if b is not None:
                        act.wait_ge(S["nb"], H * b + h + 1)
                        if h >= 2:
                            act.wait_ge(S["p_nT"], H * b + h - 1)
                        act.activation(nq[:, h % 2, :], SB_[h % 2][:, :], ACT.Exp, scale=qsc[:, 0, h:h + 1],
                                       bias=nb[:, h:h + 1], accum_out=s255[:, h:h + 1]).then_inc(S["nq"], 1)
                    run(steps, 2 * h, tiles)
                    if b is not None and h and h - 1 not in EVAC_DVE:
                        evac_nT(act, act.copy, b, h - 1)
                    run(steps, 2 * h + 1, tiles)
                if b is not None:
                    evac_nT(act, act.copy, b, H - 1)
                run(steps, 2 * H, tiles)

            sweep(act, iteration)
            act.wait_ge(S["stored"], 16 * (TILES + 1))

        @block.vector
        def _(dve):
            v = nc.vector
            n = [0]

            def link(ins, chain=None, apart=False):
                if chain is None:
                    n[0] += 1
                    ins.then_inc(S["dve_pro"], 1)
                    dve.wait_ge(S["dve_pro"], n[0])
                    return
                name, k, size, at = chain
                at[0] += 1
                ins.then_inc(S[name], 1)
                dve.wait_ge(S[name], k * size + at[0])
                if apart:
                    v.memset(spare[:, :], 0.0)

            dve.wait_ge(S["ld_wctx"], 16 * NLD)
            v.tensor_copy(identb[:, :], ident[:, :]).then_inc(S["identb"], 1)
            dve.wait_ge(S["stored"], 16)
            link(v.tensor_scalar(rs[:, :], rs[:, :], 0.0, 0.3, ALU.max, ALU.min))
            link(v.tensor_scalar(bors[:, :], rowb[:, BO0, :], rs[:, 0:1], None, ALU.mult))
            link(v.tensor_copy(ehi[:, :], maski[:, :]))
            link(v.tensor_scalar(ehi[:, :], ehi[:, :], 0.5, None, ALU.is_gt))
            link(v.tensor_scalar(ehi[:, :], ehi[:, :], E50, EM50, ALU.mult, ALU.add))
            link(v.tensor_scalar(rowb[:, BQ1, :], rowb[:, BQ1, :], 0.25, None, ALU.mult))
            dve.wait_ge(S["consts"], 6)
            with dve.Fori(0, TILES) as t:
                T = ("dve_ctx", t, 9, [0])
                dve.wait_ge(S["pv0"], t + 1)
                v.tensor_tensor(v0all[:, bass.ds(t, 1), :, 0:HD], ob[:, 0:D].rearrange("p (a h d) -> p a h d", a=1, d=HD),
                                rowb[:, BV0, :].rearrange("p (a h d) -> p a h d", a=1, d=HD),
                                ALU.add).then_inc(S["v0_done"], 1)
                dve.wait_ge(S["pk1"], t + 1)
                link(v.tensor_tensor(kf[:, :], s0[:, 0:D], rowb[:, BK1, :], ALU.add), T)
                kf3 = kf[:, :].rearrange("p (h d) -> p h d", d=HD)
                kr3 = kr1[:, :].rearrange("p (h d) -> p h d", d=HD)
                link(v.tensor_reduce(kam[:, :], kf3, AX.X, ALU.max, apply_absolute_value=True), T)
                link(v.tensor_scalar(kam[:, :], kam[:, :], 1.0 / 127.0, 1e-8, ALU.mult, ALU.max), T)
                link(v.reciprocal(krs[:, :], kam[:, :]), T)
                link(v.tensor_tensor(kf3, kf3, krs[:, :].unsqueeze(2).to_broadcast([P, H, HD]), ALU.mult), T)
                link(v.tensor_scalar(kf[:, :], kf[:, :], MAGIC, MAGIC, ALU.add, ALU.subtract), T)
                link(v.tensor_tensor(kf3, kf3, kam[:, :].unsqueeze(2).to_broadcast([P, H, HD]), ALU.mult), T)
                v.tensor_copy(kst[:, :, 0, :], kf3).then_inc(S["kst_part"], 1)
                dve.wait_ge(S["kst_part"], 3 * t + 1)
                link(v.tensor_tensor(kr3, kf3, kst[:, :, 0, :], ALU.subtract), T)
                v.tensor_copy(kst[:, :, 1, :], kr3).then_inc(S["kst_part"], 1)
                dve.wait_ge(S["kst_part"], 3 * t + 2)
                link(v.tensor_tensor(kr3, kr3, kst[:, :, 1, :], ALU.subtract), T)
                v.tensor_copy(kst[:, :, 2, :], kr3).then_inc(S["kst_part"], 1)

            dve.wait_ge(S["v1t_done"], 2 * TILES)
            link(v.tensor_reduce(vam[:, :], v1t[:, :, :], AX.X, ALU.max, apply_absolute_value=True))
            link(v.tensor_scalar(vsc[:, :], vam[:, :], 1.0 / 127.0, 1e-8, ALU.mult, ALU.max))
            link(v.reciprocal(vrs[:, :], vsc[:, :]))
            for m in range(KD):
                link(v.tensor_scalar(v1t[:, m, :], v1t[:, m, :], vrs[:, m:m + 1], MAGIC, ALU.mult, ALU.add))
                v.tensor_scalar(v1q[:, m, :], v1t[:, m, :], MAGIC, None, ALU.subtract).then_inc(S["v1q"], 1)
            dve.wait_ge(S["p_asum"], 1)
            link(v.tensor_scalar(wsc[:, :], ob[:, 0:3], 1.0 / (F1 * D), 1e-5, ALU.mult, ALU.max))
            link(v.reciprocal(wrs[:, :], wsc[:, :]))
            for i in range(3):
                link(v.tensor_scalar(wraw[:, i, :], wraw[:, i, :], wrs[:, i:i + 1], 1.0, ALU.mult, ALU.min))
                link(v.tensor_scalar(wraw[:, i, :], wraw[:, i, :], -1.0, MAGIC, ALU.max, ALU.add))
                v.tensor_scalar(tern[:, i, :], wraw[:, i, :], MAGIC, None, ALU.subtract).then_inc(S["tern"], 1)

            at = {"a": [0], "c": [0]}

            def A(k):
                return ("dve_a", k, LINKS["a"], at["a"])

            def C(k):
                return ("dve_c", k, LINKS["c"], at["c"])

            def stats(src, six, mean_var, var_eps, number, T):
                link(v.bn_stats(six[:, :], src), T, apart=True)
                link(v.bn_aggr(mean_var[:, :], six[:, :]), T)
                v.tensor_scalar(var_eps[:, :], mean_var[:, 1:2], 1e-5, None,
                                ALU.add).then_inc(S["var%d" % number], 1)

            def normed(dst, src, mean_var, rstd_, number, ready):
                def step(k):
                    dve.wait_ge(S["rstd%d" % number], k + 1)
                    v.tensor_scalar(dst[:, :], src, mean_var[:, 0:1], rstd_[:, 0:1], ALU.subtract,
                                    ALU.mult).then_inc(S[ready], 1)
                return step

            def st1(k):
                dve.wait_ge(S["ld_x"], 16 * k + 16)
                stats(xin[:, 0, :], st6, mv, ve, 1, A(k))

            def q(k):
                dve.wait_ge(S["p_qT"], k + 1)
                for m in range(KD):
                    v.scalar_tensor_tensor(
                        qbd[:, m, :, :], fB[:, m * P:(m + 1) * P].unsqueeze(1).to_broadcast([P, 8, P]),
                        colb[:, 0, m:m + 1], headmask[:, :].unsqueeze(2).to_broadcast([P, 8, P]),
                        ALU.add, ALU.mult).then_inc(S["qbd"], 1)

            def sc(j0):
                def step(k):
                    for j in (j0, j0 + 1):
                        h4, kt = 4 * (j // 2), j % 2
                        dve.wait_ge(S["e0"], 8 * k + j + 1)
                        v.tensor_scalar(e0[:, kt, h4:h4 + 4, :], e0[:, kt, h4:h4 + 4, :],
                                        ehi[:, bass.ds((k // 2) * 2 + kt, 1)], EM50, ALU.min,
                                        ALU.max).then_inc(S["e0c"], 1)
                return step

            def cx1(k):
                dve.wait_ge(S["p_ctx"], k + 1)
                c3 = fA[:, 0:H * (HD + 1)].rearrange("p (h d) -> p h d", d=HD + 1)
                link(v.reciprocal(den0[:, :], c3[:, :, HD]), A(k))
                v.tensor_tensor(ctx0[:, :, :], c3[:, :, 0:HD], den0[:, :].unsqueeze(2).to_broadcast([P, H, HD]),
                                ALU.mult).then_inc(S["ctx0"], 1)

            def dlt(k):
                dve.wait_ge(S["p_dl"], k + 1)
                v.scalar_tensor_tensor(dl[:, :], fA[:, 0:D], rs[:, 0:1], bors[:, :], ALU.mult,
                                       ALU.add).then_inc(S["dl"], 1)
                dve.wait_ge(S["dl"], k + 1)
                stats(dl[:, :], st6, mv, ve, 2, A(k))

            def xone(k):
                dve.wait_ge(S["rstd2"], k + 1)
                link(v.scalar_tensor_tensor(dl[:, :], dl[:, :], mv[:, 0:1], rowb[:, GAM, :], ALU.subtract,
                                            ALU.mult), A(k))
                dve.wait_ge(S["xb_ready"], k + 1)
                v.scalar_tensor_tensor(x1[:, :], dl[:, :], rstd[:, 0:1], xb[:, :], ALU.mult,
                                       ALU.add).then_inc(S["xin_free"], 1)
                dve.wait_ge(S["xin_free"], k + 1)
                stats(x1[:, :], st6, mv, ve, 3, A(k))

            def ul(k):
                T = A(k)
                dve.wait_ge(S["p_ul"], k + 1)
                link(v.tensor_copy(lg[:, :], fA[:, 2 * P:2 * P + E]), T, apart=True)
                link(v.max(top[:, :], lg[:, :]), T)
                v.tensor_tensor(dm[:, :], top[:, 1:2], top[:, 0:1], ALU.subtract).then_inc(S["dmax"], 1)
                link(v.max_index(topi[:, :], top[:, :], lg[:, :]), T)
                link(v.tensor_copy(topf[:, :], topi[:, 0:2]), T)
                for s in range(2):
                    link(v.tensor_scalar(oh[:, s, :], iota8[:, :], topf[:, s:s + 1], LORA, ALU.is_equal,
                                         ALU.mult), T)
                u4 = fA[:, 0:2 * P].rearrange("p (a e r) -> p a e r", a=2, e=E)
                for s in range(2):
                    link(v.tensor_tensor(us[:, s, :, :, :], u4,
                                         oh[:, s, :].unsqueeze(1).unsqueeze(3).to_broadcast([P, 2, E, R]),
                                         ALU.mult), T)
                v.tensor_tensor(us[:, 1, :, :, :], us[:, 1, :, :, :], us[:, 0, :, :, :],
                                ALU.subtract).then_inc(S["us"], 1)

            def route(k):
                T = A(k)
                dve.wait_ge(S["em"], k + 1)
                link(v.tensor_scalar(em1[:, :], em[:, :], 1.0, None, ALU.add), T)
                link(v.reciprocal(rw[:, 0:1], em1[:, :]), T)
                link(v.tensor_tensor(rw[:, 1:2], rw[:, 0:1], em[:, :], ALU.mult), T)
                link(v.tensor_scalar(rw[:, :], rw[:, :], 0.5, None, ALU.mult), T)

            def gated(i):
                j, s = i // 2, i % 2

                def step(k):
                    dve.wait_ge(S["th"], 4 * k + i + 1)
                    if i:
                        dve.wait_ge(S["aw"], 4 * k + i)
                    v.scalar_tensor_tensor(gs[:, :], th[:, :], 1.0, fA[:, 0:FH], ALU.add,
                                           ALU.mult).then_inc(S["gs"], 1)
                    dve.wait_ge(S["gs"], 4 * k + i + 1)
                    dve.wait_ge(S["p_h3"], 4 * k + i + 1)
                    v.scalar_tensor_tensor(aw[:, s, j * FH:(j + 1) * FH], gs[:, :], rw[:, s:s + 1],
                                           fB[:, 0:FH], ALU.mult, ALU.mult).then_inc(S["aw"], 1)
                return step

            def z(k):
                dve.wait_ge(S["p_z"], k + 1)
                link(v.tensor_tensor(zz[:, :, :].rearrange("p s (e r) -> p (s e) r", r=R),
                                     fB[:, 0:2 * P].rearrange("p (e r) -> p e r", r=R),
                                     oh[:, :, :].rearrange("p s e -> p (s e)").unsqueeze(2).to_broadcast([P, 2 * E, R]),
                                     ALU.mult), A(k))
                v.tensor_tensor(zm[:, :], zz[:, 0, :], zz[:, 1, :], ALU.add).then_inc(S["zm"], 1)

            def y(k):
                dve.wait_ge(S["p_y"], k + 1)
                if ints(k) != 0:
                    dve.wait_ge(S["x2b_ready"], k)
                v.tensor_tensor(x2[:, :], fB[:, 0:D], x1[:, :], ALU.add).then_inc(S["x2_ready"], 1)
                dve.wait_ge(S["x2_ready"], k + 1)
                stats(x2[:, :], st6, mv, ve, 4, A(k))

            def qone(k):
                T = A(k)
                dve.wait_ge(S["p_q1"], k + 1)
                v.scalar_tensor_tensor(qf[:, :], fB[:, 0:D], 0.25, rowb[:, BQ1, :], ALU.mult,
                                       ALU.add).then_inc(S["qf"], 1)
                dve.wait_ge(S["qf"], k + 1)
                qf3 = qf[:, :].rearrange("p (h d) -> p h d", d=HD)
                link(v.tensor_reduce(qam[:, :], qf3, AX.X, ALU.max, apply_absolute_value=True), T)
                link(v.tensor_scalar(qsc_n[:, 0, :], qam[:, :], 1.0 / 127.0, 1e-8, ALU.mult, ALU.max), T)
                link(v.tensor_scalar(qsc_n[:, 1, :], qsc_n[:, 0, :], -1.0, None, ALU.mult), T)
                link(v.reciprocal(qrs[:, :], qsc_n[:, 0, :]), T)
                link(v.tensor_tensor(qf3, qf3, qrs[:, :].unsqueeze(2).to_broadcast([P, H, HD]), ALU.mult), T)
                v.tensor_scalar(qst[:, :, 0:3, :], qf3.unsqueeze(2).to_broadcast([P, H, 3, HD]), MAGIC, MAGIC,
                                ALU.add, ALU.subtract).then_inc(S["qst"], 1)

            def o1div(k):
                dve.wait_ge(S["nq"], H * k + H)
                link(v.reciprocal(r255[:, :], s255[:, :]), C(k))
                dve.wait_ge(S["p_pv"], H * k + H)
                v.tensor_tensor(o1[:, :, :], ob[:, 0:D].rearrange("p (h d) -> p h d", d=HD),
                                r255[:, :].unsqueeze(2).to_broadcast([P, H, HD]), ALU.mult).then_inc(S["o1"], 1)

            def d2(k):
                dve.wait_ge(S["p_d2"], k + 1)
                dve.wait_ge(S["x2b_ready"], k + 1)
                v.tensor_tensor(x3[:, :], fB[:, 0:D], x2b[:, :], ALU.add).then_inc(S["x3"], 1)
                dve.wait_ge(S["x3"], k + 1)
                stats(x3[:, :], bst6, bmv, bve, 5, C(k))

            def xn4(k):
                T = C(k)
                normed(bxn, x3[:, :], bmv, brstd, 5, "xn4")(k)
                dve.wait_ge(S["xn4"], k + 1)
                link(v.tensor_reduce(xam[:, :], bxn[:, :], AX.X, ALU.max, apply_absolute_value=True), T)
                link(v.tensor_scalar(xam[:, :], xam[:, :], 1e-5, 1.0 / 127.0, ALU.max, ALU.mult), T)
                link(v.reciprocal(xrs[:, :], xam[:, :]), T)
                link(v.tensor_scalar(bxn[:, :], bxn[:, :], xrs[:, 0:1], MAGIC, ALU.mult, ALU.add), T)
                v.tensor_scalar(xi[:, :], bxn[:, :], MAGIC, None, ALU.subtract).then_inc(S["xi"], 1)
                link(v.tensor_tensor(al[:, 0:1], xam[:, :], wsc[:, 0:1], ALU.mult), T)
                link(v.tensor_tensor(al[:, 2:3], xam[:, :], wsc[:, 1:2], ALU.mult), T)
                v.tensor_scalar(al[:, 1:2], al[:, 0:1], 0.5, None, ALU.mult).then_inc(S["al"], 1)
                dve.wait_ge(S["al"], k + 1)
                link(v.tensor_tensor(sq[:, 0:1], al[:, 1:2], al[:, 2:3], ALU.mult), T)
                link(v.tensor_tensor(sq[:, 2:3], sq[:, 0:1], sq[:, 0:1], ALU.mult), T)

            def gu(k):
                dve.wait_ge(S["bth"], k + 1)
                v.scalar_tensor_tensor(hg[:, :], bth[:, :], 1.0, s0[:, :], ALU.add, ALU.mult).then_inc(S["hg"], 1)
                dve.wait_ge(S["hg"], k + 1)
                dve.wait_ge(S["p_u"], k + 1)
                v.tensor_tensor(hg[:, :], hg[:, :], s1[:, :], ALU.mult).then_inc(S["hu"], 1)

            def rms(k):
                T = C(k)
                dve.wait_ge(S["hu"], k + 1)
                link(v.scalar_tensor_tensor(bth[:, :], hg[:, :], 1.0, hg[:, :], ALU.mult, ALU.mult,
                                            accum_out=sq[:, 1:2]), T)
                link(v.tensor_tensor(sq[:, 2:3], sq[:, 2:3], sq[:, 1:2], ALU.mult), T)
                v.tensor_scalar(bve[:, :], sq[:, 2:3], 1.0 / F1, 1e-6, ALU.mult, ALU.add).then_inc(S["var6"], 1)

            def hmax(k):
                T = C(k)
                link(v.tensor_tensor(hr[:, :], hg[:, :], lnw[:, :], ALU.mult), T)
                link(v.tensor_reduce(sq[:, 3:4], hr[:, :], AX.X, ALU.max, apply_absolute_value=True), T)

            def hint(k):
                T = C(k)
                dve.wait_ge(S["rstd6"], k + 1)
                link(v.tensor_tensor(sq[:, 4:5], brstd[:, :], sq[:, 0:1], ALU.mult), T)
                link(v.tensor_tensor(sq[:, 5:6], sq[:, 3:4], sq[:, 4:5], ALU.mult), T)
                link(v.tensor_scalar(sq[:, 5:6], sq[:, 5:6], 1e-5, 1.0 / 127.0, ALU.max, ALU.mult), T)
                link(v.reciprocal(sq[:, 6:7], sq[:, 5:6]), T)
                link(v.tensor_tensor(sq[:, 6:7], sq[:, 6:7], sq[:, 4:5], ALU.mult), T)
                link(v.tensor_scalar(hr[:, :], hr[:, :], sq[:, 6:7], MAGIC, ALU.mult, ALU.add), T)
                v.tensor_scalar(hi[:, :], hr[:, :], MAGIC, None, ALU.subtract).then_inc(S["hi"], 1)
                link(v.tensor_tensor(sq[:, 7:8], sq[:, 5:6], wsc[:, 2:3], ALU.mult), T)

            def y1(k):
                dve.wait_ge(S["p_y1"], k + 1)
                dve.wait_ge(S["stored"], 16 * k + 16)
                v.scalar_tensor_tensor(yo[:, :], fA[:, 0:D], sq[:, 7:8], x3[:, :], ALU.mult,
                                       ALU.add).then_inc(S["yo_ready"], 1)

            steps = {"a_st1": st1, "a_xn1": normed(xn, xin[:, 0, :], mv, rstd, 1, "xn1"), "a_q": q,
                     "a_sc0": sc(0), "a_sc1": sc(2), "a_sc2": sc(4), "a_sc3": sc(6), "a_cx1": cx1,
                     "a_dl": dlt, "a_x1": xone, "a_xn2": normed(xn, x1[:, :], mv, rstd, 3, "xn2"),
                     "a_ul": ul, "a_us": route, "a_h00": gated(0), "a_h01": gated(1), "a_h10": gated(2),
                     "a_h11": gated(3), "a_z": z, "a_y": y,
                     "a_xn3": normed(xn, x2[:, :], mv, rstd, 4, "xn3"), "a_q1": qone,
                     "c_d2": d2, "c_xn4": xn4, "c_gu": gu, "c_rms": rms, "c_hmax": hmax, "c_hi": hint,
                     "c_y1": y1}

            def iteration(tiles):
                at["a"][0] = at["c"][0] = 0
                b = tiles["b"]
                if tiles["c"] is not None:
                    o1div(tiles["c"])
                if b is not None:
                    dve.wait_ge(S["qiT_n"], b + 1)
                    v.tensor_copy(qiT[:, :, :], qiT_n[:, :, :]).then_inc(S["q_here"], 1)
                    v.tensor_copy(qsc[:, :, :], qsc_n[:, :, :]).then_inc(S["q_here"], 1)
                    dve.wait_ge(S["q_here"], 2 * b + 2)
                for h in range(H):
                    if b is not None:
                        dve.wait_ge(S["p_s"], H * b + h + 1)
                        v.tensor_reduce(mx[:, h:h + 1], SB_[h % 2][:, :], AX.X, ALU.max).then_inc(S["mx"], 1)
                        dve.wait_ge(S["mx"], H * b + h + 1)
                        v.tensor_scalar(nb[:, h:h + 1], mx[:, h:h + 1], qsc[:, 1, h:h + 1], LN255, ALU.mult,
                                        ALU.add).then_inc(S["nb"], 1)
                    run(steps, 2 * h, tiles)
                    if b is not None and h and h - 1 in EVAC_DVE:
                        evac_nT(dve, v.tensor_copy, b, h - 1)
                    run(steps, 2 * h + 1, tiles)
                run(steps, 2 * H, tiles)
                for s in "ac":
                    if tiles[s] is not None:
                        assert at[s][0] == LINKS[s], (s, at[s][0])

            sweep(dve, iteration)

        @block.tensor
        def _(pe):
            mm = nc.tensor.matmul
            tr = nc.tensor.transpose

            def proj(outs, lhs, rhs):
                for k in range(KD):
                    i = mm(outs, lhs(k), rhs(k), start=(k == 0), stop=(k == KD - 1))
                return i

            pe.wait_ge(S["ld_wctx"], 16 * NLD)
            pe.wait_ge(S["identb"], 1)
            pe.wait_ge(S["consts"], 6)
            with pe.Fori(0, TILES // 2) as u:
                for s in range(2):
                    pe.wait_ge(S["ld_ctx%d" % s], 16 * u + 16)
                    c = ctxt[:, s]
                    tt = 2 * u + s
                    for m in range(KD):
                        i = proj(fA[:, m * P:(m + 1) * P], lambda k: wk0[:, k, m * P:(m + 1) * P], lambda k: c[:, k, :])
                    i.then_inc(S["pk0"], 1)
                    for m in range(KD):
                        i = proj(fB[:, m * P:(m + 1) * P], lambda k: wkv1[:, k, D + m * P:D + (m + 1) * P], lambda k: c[:, k, :])
                    i.then_inc(S["pv1"], 1)
                    proj(ob[:, 0:D], lambda k: c[:, k, :], lambda k: wv0[:, k, :]).then_inc(S["pv0"], 1)
                    proj(s0[:, 0:D], lambda k: c[:, k, :], lambda k: wkv1[:, k, 0:D]).then_inc(S["pk1"], 1)
                    pe.wait_ge(S["kst_part"], 3 * tt + 3)
                    for g in range(8):
                        i = tr(tb[:, g, :], kst[:, 2 * g:2 * g + 2, :, :].rearrange("p a b c -> p (a b c)"), identb[:, :])
                    i.then_inc(S["pk1T"], 1)
                    pe.wait_ge(S["k0_done"], 2 * tt + 2)
                    pe.wait_ge(S["v1t_done"], 2 * tt + 2)
                    pe.wait_ge(S["v0_done"], tt + 1)
                    pe.wait_ge(S["k1T_done"], tt + 1)
            pe.wait_ge(S["asum"], 3)
            mm(ob[:, 0:3], ones[:, :], asum[:, :], start=True, stop=True).then_inc(S["p_asum"], 1)
            for m in range(KD):
                pe.wait_ge(S["v1q"], m + 1)
                if m:
                    pe.wait_ge(S["v1i_done"], m)
                for k in range(KT):
                    i = tr(tb[:, k, :], v1q[:, m, k * P:(k + 1) * P], identb[:, :])
                i.then_inc(S["pv1iT"], 1)
            pe.wait_ge(S["v1i_done"], KD)
            pe.wait_ge(S["tern"], 3)
            pe.wait_ge(S["ld_w"], 16 * 10)

            wl = [P] * (FC - 1) + [FL]
            read_when = {}

            def take(bk):
                if bk in read_when:
                    pe.wait_ge(*read_when.pop(bk))

            def give(bk, name, value):
                read_when[bk] = (S[name], value)

            def turn(name, src, ready, full, done):
                def step(k):
                    bk = {"fA": fA, "fB": fB}[name]
                    pe.wait_ge(S[ready], k + 1)
                    take(name)
                    for c in range(KD):
                        i = tr(bk[:, c * P:(c + 1) * P], src[:, c * P:(c + 1) * P], ident[:, :])
                    i.then_inc(S[full], 1)
                    give(name, done, (2 if done == "oT" else 1) * (k + 1))
                return step

            def q(k):
                pe.wait_ge(S["xT1"], k + 1)
                take("fB")
                for m in range(KD):
                    i = proj(fB[:, m * P:(m + 1) * P], lambda c: wq0[:, c, m * P:(m + 1) * P], lambda c: xT[:, c, :])
                i.then_inc(S["p_qT"], 1)
                give("fB", "qbd", 2 * k + 2)

            def sc(j0):
                def step(k):
                    if j0 == 0:
                        pe.wait_ge(S["kv_ready"], 2 * k + 2)
                        pe.wait_ge(S["qbd"], 2 * k + 2)
                    for j in (j0, j0 + 1):
                        m, half, kt, name = j // 4, (j // 2) % 2, j % 2, ("fA", "fB")[j % 2]
                        take(name)
                        mm((fA, fB)[j % 2][:, 0:512], kcur[:, m, kt * P:(kt + 1) * P],
                           qbd[:, m, 4 * half:4 * half + 4, :], start=True, stop=True).then_inc(S["p_sc"], 1)
                        give(name, "e0", 8 * k + j + 1)
                return step

            def cx(half):
                def step(k):
                    pe.wait_ge(S["e0c"], 8 * k + 4 + 4 * half)
                    take("fA")
                    for h in range(8 * half, 8 * half + 8):
                        for kt in range(2):
                            i = mm(fA[:, h * (HD + 1):(h + 1) * (HD + 1)], e0[:, kt, h, :], vcur[:, kt, h, :],
                                   start=(kt == 0), stop=(kt == 1))
                    if half:
                        i.then_inc(S["p_ctx"], 1)
                        give("fA", "ctx0", k + 1)
                return step

            def dlt(k):
                pe.wait_ge(S["cT"], k + 1)
                take("fA")
                proj(fA[:, 0:D], lambda c: cT[:, c, :], lambda c: wo0[:, c, :]).then_inc(S["p_dl"], 1)
                give("fA", "dl", k + 1)

            def ul(k):
                pe.wait_ge(S["xT2"], k + 1)
                take("fA")
                proj(fA[:, 0:2 * P + E], lambda c: xT[:, c, :], lambda c: a13g[:, c, :]).then_inc(S["p_ul"], 1)
                give("fA", "us", k + 1)

            def usr(k):
                pe.wait_ge(S["us"], k + 1)
                take("fB")
                for s in range(2):
                    for p in range(2):
                        i = tr(fB[:, (2 * s + p) * P:(2 * s + p + 1) * P],
                               us[:, s, p, :, :].rearrange("p e r -> p (e r)"), ident[:, :])
                i.then_inc(S["p_usT"], 1)
                give("fB", "usT", k + 1)

            def gated(n):
                j, s = n // 2, n % 2

                def step(k):
                    pe.wait_ge(S["usT"], k + 1)
                    for p in range(2):
                        bk, name, col = (fA, fB)[p], ("fA", "fB")[p], p * F0 + j * FH
                        take(name)
                        if s == 0:
                            for c in range(KD):
                                mm(bk[:, 0:FH], xT[:, c, :], w13[:, c, col:col + FH], start=(c == 0), stop=False,
                                   skip_group_check=True)
                        mm(bk[:, 0:FH], usT[:, 2 * s + p, :], b13[:, col:col + FH], start=False, stop=(s == 1),
                           skip_group_check=True).then_inc(S[("p_h1", "p_h3")[p]], 1)
                        give(name, ("gs", "aw")[p], 4 * k + n + 1)
                return step

            def awt(k):
                pe.wait_ge(S["aw"], 4 * k + 4)
                for s in range(2):
                    take(("fA", "fB")[s])
                    for c in range(4):
                        i = tr((fA, fB)[s][:, c * P:(c + 1) * P], aw[:, s, c * P:(c + 1) * P], ident[:, :])
                    i.then_inc(S["p_awT"], 1)
                    give(("fA", "fB")[s], "awT_ready", 4 * k + s + 1)
                take("fA")
                for c in (4, 5):
                    for s in range(2):
                        w = wl[c]
                        i = tr(fA[0:w, ((c - 4) * 2 + s) * P:((c - 4) * 2 + s + 1) * P],
                               aw[:, s, c * P:c * P + w], ident[:, :])
                i.then_inc(S["p_awT"], 1)
                give("fA", "awT_ready", 4 * k + 4)

            def z(k):
                pe.wait_ge(S["awT_ready"], 4 * k + 4)
                take("fB")
                for s in range(2):
                    for c in range(FC):
                        i = mm(fB[:, s * P:(s + 1) * P], awT[0:wl[c], s, c, :], w2a2[0:wl[c], c, D:D + P],
                               start=(c == 0), stop=(c == FC - 1))
                i.then_inc(S["p_z"], 1)
                give("fB", "zm", k + 1)

            def y(k):
                pe.wait_ge(S["zm"], k + 1)
                take("fA")
                tr(fA[:, 0:P], zm[:, :], ident[:, :]).then_inc(S["p_zT"], 1)
                give("fA", "zT", k + 1)
                pe.wait_ge(S["gT_ready"], 2 * k + 2)
                take("fB")
                for c in range(FC):
                    mm(fB[:, 0:D], gT[0:wl[c], c, :], w2a2[0:wl[c], c, 0:D], start=(c == 0), stop=False)
                pe.wait_ge(S["zT"], k + 1)
                mm(fB[:, 0:D], zT[:, :], b2[:, :], start=False, stop=True).then_inc(S["p_y"], 1)
                give("fB", "x2_ready", k + 1)

            def qone(k):
                pe.wait_ge(S["bxT"], k + 1)
                take("fB")
                proj(fB[:, 0:D], lambda c: bxT[:, c, :], lambda c: wq1[:, c, :]).then_inc(S["p_q1"], 1)
                give("fB", "qf", k + 1)

            def turn_tb(count, src, ready, full, done):
                def step(k):
                    pe.wait_ge(S[ready], k + 1)
                    take("tb")
                    for c in range(count):
                        i = tr(tb[:, c, :], src(c), identb[:, :])
                    i.then_inc(S[full], 1)
                    give("tb", done, k + 1)
                return step

            def d2(k):
                pe.wait_ge(S["oT"], 2 * k + 2)
                take("fB")
                proj(fB[:, 0:D], lambda c: oT[:, c, :], lambda c: wp1[:, c, :]).then_inc(S["p_d2"], 1)
                give("fB", "x3", k + 1)

            def bitlinear(g, k):
                for c in range(2):
                    for d in range(KD):
                        i = mm(SB_[g][:, c * 512:(c + 1) * 512], xiT[:, d, :],
                               tern[:, g, d * F1 + c * 512:d * F1 + (c + 1) * 512],
                               start=(d == 0), stop=(d == KD - 1))
                i.then_inc(S[("p_g", "p_u")[g]], 1)

            def y1(k):
                pe.wait_ge(S["hiT"], k + 1)
                take("fA")
                for c in range(8):
                    i = mm(fA[:, 0:D], hiT[:, c, :], tern[:, 2, c * D:(c + 1) * D], start=(c == 0), stop=(c == 7))
                i.then_inc(S["p_y1"], 1)
                give("fA", "yo_ready", k + 1)

            steps = {"a_xn1": turn("fA", xn, "xn1", "p_xT1", "xT1"), "a_q": q,
                     "a_sc0": sc(0), "a_sc1": sc(2), "a_sc2": sc(4), "a_sc3": sc(6),
                     "a_cx0": cx(0), "a_cx1": cx(1),
                     "a_cT": turn("fB", ctx0[:, :, :].rearrange("p h d -> p (h d)"), "ctx0", "p_cT", "cT"),
                     "a_dl": dlt, "a_xn2": turn("fB", xn, "xn2", "p_xT2", "xT2"), "a_ul": ul, "a_us": usr,
                     "a_h00": gated(0), "a_h01": gated(1), "a_h10": gated(2), "a_h11": gated(3),
                     "a_awT": awt, "a_z": z, "a_y": y, "a_xn3": turn("fA", xn, "xn3", "p_xT3", "bxT"),
                     "a_q1": qone,
                     "a_qiT": turn_tb(8, lambda g: qst[:, 2 * g:2 * g + 2, :, :].rearrange("p a b c -> p (a b c)"),
                                      "qst", "p_qiT", "qiT_n"),
                     "c_oT": turn("fB", o1.rearrange("p h d -> p (h d)"), "o1", "p_oT", "oT"), "c_d2": d2,
                     "c_xiT": turn_tb(KD, lambda c: xi[:, c * P:(c + 1) * P], "xi", "p_xiT", "xiT"),
                     "c_hiT": turn_tb(8, lambda c: hi[:, c * P:(c + 1) * P], "hi", "p_hiT", "hiT"), "c_y1": y1}

            def scores(b, h, c):
                if h >= 2:
                    pe.wait_ge(S["nq"], H * b + h - 1)
                if c is not None and h in (8, 9):
                    pe.wait_ge(S[("hg", "hu")[h - 8]], c + 1)
                lo = 64 * (h % 2)
                for n in range(2):
                    i = mm(SB_[h % 2][:, n * 512:(n + 1) * 512], qiT[lo:lo + 64, h // 2, :],
                           k1t[lo:lo + 64, h // 2, n * 512:(n + 1) * 512], start=True, stop=True)
                i.then_inc(S["p_s"], 1)

            def turn_n(b, h):
                pe.wait_ge(S["nq"], H * b + h + 1)
                take("tb")
                src = nq[:, h % 2, :].bitcast(BF16)
                for k in range(KT):
                    i = tr(tb[:, k, :], src[:, k * P:(k + 1) * P], identb[:, :])
                i.then_inc(S["p_nT"], 1)
                give("tb", "nT", H * b + h + 1)

            def weigh(b, h):
                pe.wait_ge(S["nT"], H * b + h + 1)
                for k in range(KT):
                    i = mm(ob[:, h * HD:(h + 1) * HD], nT[:, h % 2, k, :], v1i[:, k, h * HD:(h + 1) * HD],
                           start=(k == 0), stop=(k == KT - 1))
                i.then_inc(S["p_pv"], 1)

            def iteration(tiles):
                b, c = tiles["b"], tiles["c"]
                if b is not None:
                    pe.wait_ge(S["q_here"], 2 * b + 2)
                    scores(b, 0, c)
                    scores(b, 1, c)
                for h in range(H):
                    run(steps, 2 * h, tiles)
                    if b is not None:
                        if h == 8 and c is not None:
                            scores(b, 9, c)
                        turn_n(b, h)
                    if h in (6, 7) and c is not None:
                        if b is not None:
                            pe.wait_ge(S["nq"], H * b + h + 1)
                        if h == 6:
                            pe.wait_ge(S["xiT"], c + 1)
                        bitlinear(h - 6, c)
                    elif b is not None and h + 2 < H:
                        scores(b, h + 2, c)
                    run(steps, 2 * h + 1, tiles)
                    if b is not None:
                        if h:
                            weigh(b, h - 1)
                        if h == 7 and c is not None:
                            scores(b, 8, c)
                if b is not None:
                    weigh(b, H - 1)
                run(steps, 2 * H, tiles)
                for bk in ("fA", "fB", "tb"):
                    take(bk)

            sweep(pe, iteration)


def ints(k):
    return k if isinstance(k, int) else None


LINKS = {"a": 28, "c": 22}
EVAC_DVE = (0, 2, 4, 6, 8, 10, 12, 14)
POINTS = 2 * H + 1
PLAN = {p: [] for p in range(POINTS)}
for _point, _names in {
    0: "a_st1 b_x2b", 1: "a_xn1 c_oT", 2: "a_q", 3: "c_d2", 4: "a_sc0", 5: "a_sc1 c_xn4", 6: "a_sc2", 7: "a_sc3",
    8: "a_cx0", 9: "a_cx1", 10: "a_cT c_xiT", 11: "a_dl", 12: "a_x1", 13: "a_xn2", 14: "a_ul",
    15: "c_gu", 16: "a_us", 17: "a_h00", 18: "a_h01 c_rms", 19: "a_h10 c_hmax", 20: "a_h11", 21: "a_awT c_hi",
    22: "c_hiT", 23: "a_z", 24: "c_y1", 25: "a_y", 26: "c_st", 27: "a_xn3", 29: "a_q1", 30: "a_qiT",
}.items():
    PLAN[_point] = _names.split()




def lay_out(inputs):
    import numpy as np
    g = {k: np.asarray(v) for k, v in inputs.items()}

    def rows(w):
        return np.ascontiguousarray(w.reshape(-1, P, w.shape[1]).transpose(1, 0, 2))

    er = lambda w: w.reshape(E * R, -1)
    w2a2 = np.zeros((FC * P, D + P), np.float32)
    w2a2[:F0, :D] = g["L0_ffn_w2"].T
    w2a2[:F0, D:] = er(g["L0_ffn_a2"]).T
    col = lambda b: b.reshape(KD, P).T
    kv = g["L1_xattn_bkv"]
    hm = np.zeros((P, 8), np.float32)
    hm[np.arange(P), np.arange(P) // HD] = float(HD) ** -0.5
    arrays = {
        "x": g["x"].reshape(N_TOK, D),
        "ctxt": g["ctx_2048"].reshape(TILES, P, KD, P).transpose(0, 3, 2, 1),
        "ident": np.eye(P, dtype=np.float32),
        "headmask": hm,
        "iota8": np.tile(np.arange(E, dtype=np.float32), (P, 1)),
        "maski": g["mask_BxS2_ik0"].reshape(8, P).T,
        "wq0": rows(g["L0_xattn_Wq"].T), "wk0": rows(g["L0_xattn_Wk"].T),
        "wv0": rows(g["L0_xattn_Wv"].T), "wo0": rows(g["L0_xattn_Wo"].T),
        "wq1": rows(g["L1_xattn_Wq"]), "wkv1": rows(g["L1_xattn_Wkv"]), "wp1": rows(g["L1_xattn_Wp"]),
        "a13g": rows(np.concatenate([er(g["L0_ffn_a1"]).T, er(g["L0_ffn_a3"]).T, g["L0_ffn_gate_w"].T], 1)),
        "w13": rows(np.concatenate([g["L0_ffn_w1"].T, g["L0_ffn_w3"].T], 1)),
        "b13": np.concatenate([er(g["L0_ffn_b1"].transpose(0, 2, 1)), er(g["L0_ffn_b3"].transpose(0, 2, 1))], 1),
        "w2a2": rows(w2a2),
        "b2": er(g["L0_ffn_b2"].transpose(0, 2, 1)),
        "colb": np.stack([col(g["L0_xattn_bq"]), col(g["L0_xattn_bk"]), col(kv[D:])], 1),
        "bv0": g["L0_xattn_bv"], "bo0": g["L0_xattn_bo"], "gamma": g["L0_xattn_ln_gamma"],
        "beta": g["L0_xattn_ln_beta"], "bq1": g["L1_xattn_bq"], "bk1": kv[:D], "bp1": g["L1_xattn_bp"],
        "rs": g["L0_xattn_residual_scale"].reshape(1),
        "lnw": g["L1_ffn_ln_weight"],
        "wg1": rows(g["L1_ffn_w_gate"].T).reshape(P, -1), "wu1": rows(g["L1_ffn_w_up"].T).reshape(P, -1),
        "wd1": rows(g["L1_ffn_w_down"].T).reshape(P, -1),
    }
    return {k: np.ascontiguousarray(v) for k, v in arrays.items()}


def kernel(**inputs):
    import concourse.bacc as _bacc
    from concourse.bass_utils import run_bass_kernel_spmd as _run

    arrays = lay_out(inputs)
    nc = _bacc.Bacc("TRN2", target_bir_lowering=False, num_devices=1)
    aps = {k: nc.dram_tensor("in_" + k, v.shape, mybir.dt.from_np(v.dtype), kind="ExternalInput").ap()
           for k, v in arrays.items()}
    out = nc.dram_tensor("out_y", (N_TOK, D), F32, kind="ExternalOutput").ap()
    build(nc, aps, out)
    r = _run(nc, [{"in_" + k: v for k, v in arrays.items()}], core_ids=[0])
    return r.results[0]["out_y"].reshape(4, BATCH, D)
```
